# Optimizing a Trainium2 kernel written in Bass

```python
import numpy as np
import jax
import jax.numpy as jnp

def _softmax(x, axis=-1):
    return jax.nn.softmax(x, axis=axis)

def _gelu(x):
    return jax.nn.gelu(x, approximate=True)

def _silu(x):
    return jax.nn.silu(x)

def _sigmoid(x):
    return jax.nn.sigmoid(x)

def _layernorm(x, axis=-1, eps=1e-05):
    m = jnp.mean(x, axis=axis, keepdims=True)
    v = jnp.var(x, axis=axis, keepdims=True)
    return (x - m) / jnp.sqrt(v + eps)

def _scatter_add(tgt, idx, src, axis=0):
    return tgt.at[idx].add(src)

def _segment_sum(src, seg, n):
    return jax.ops.segment_sum(src, seg, n)
kernel_name = 'mk_dlrm_tower_d1_rec_r8_e8b203'

def setup_inputs(seed: int=0):
    np.random.seed(seed)
    _w = jnp.asarray

    def _rec_inputs():
        import jax
        import jax.numpy as jnp
        _tk = jax.random.key(seed)
        dense_ctx = jax.random.normal(jax.random.fold_in(_tk, 190), (512, 16), jnp.float32)
        ids = jnp.stack([jax.random.randint(jax.random.fold_in(_tk, 200 + f), (512,), 0, v, jnp.int32) for f, v in enumerate([1250, 125000, 125000, 1000, 125000, 1000, 12500, 1000, 1250, 12500, 1250, 125000, 1250, 1000, 12500, 1000, 1250, 1000, 1250, 1250, 1250, 1000, 12500, 125000, 1000, 12500, 1000, 125000, 1000, 1000, 1250, 12500, 12500, 12500, 1250, 12500, 12500, 1000, 1250, 12500, 1250, 1250, 1250, 1000, 1250, 12500, 12500, 1250])], axis=1)
        tbl_0 = 0.05 * jax.random.normal(jax.random.fold_in(_tk, 500 + 0), (1250, 32), jnp.float32)
        tbl_1 = 0.05 * jax.random.normal(jax.random.fold_in(_tk, 500 + 1), (125000, 32), jnp.float32)
        tbl_2 = 0.05 * jax.random.normal(jax.random.fold_in(_tk, 500 + 2), (125000, 32), jnp.float32)
        tbl_3 = 0.05 * jax.random.normal(jax.random.fold_in(_tk, 500 + 3), (1000, 32), jnp.float32)
        tbl_4 = 0.05 * jax.random.normal(jax.random.fold_in(_tk, 500 + 4), (125000, 32), jnp.float32)
        tbl_5 = 0.05 * jax.random.normal(jax.random.fold_in(_tk, 500 + 5), (1000, 32), jnp.float32)
        tbl_6 = 0.05 * jax.random.normal(jax.random.fold_in(_tk, 500 + 6), (12500, 32), jnp.float32)
        tbl_7 = 0.05 * jax.random.normal(jax.random.fold_in(_tk, 500 + 7), (1000, 32), jnp.float32)
        tbl_8 = 0.05 * jax.random.normal(jax.random.fold_in(_tk, 500 + 8), (1250, 32), jnp.float32)
        tbl_9 = 0.05 * jax.random.normal(jax.random.fold_in(_tk, 500 + 9), (12500, 32), jnp.float32)
        tbl_10 = 0.05 * jax.random.normal(jax.random.fold_in(_tk, 500 + 10), (1250, 32), jnp.float32)
        tbl_11 = 0.05 * jax.random.normal(jax.random.fold_in(_tk, 500 + 11), (125000, 32), jnp.float32)
        tbl_12 = 0.05 * jax.random.normal(jax.random.fold_in(_tk, 500 + 12), (1250, 32), jnp.float32)
        tbl_13 = 0.05 * jax.random.normal(jax.random.fold_in(_tk, 500 + 13), (1000, 32), jnp.float32)
        tbl_14 = 0.05 * jax.random.normal(jax.random.fold_in(_tk, 500 + 14), (12500, 32), jnp.float32)
        tbl_15 = 0.05 * jax.random.normal(jax.random.fold_in(_tk, 500 + 15), (1000, 32), jnp.float32)
        tbl_16 = 0.05 * jax.random.normal(jax.random.fold_in(_tk, 500 + 16), (1250, 32), jnp.float32)
        tbl_17 = 0.05 * jax.random.normal(jax.random.fold_in(_tk, 500 + 17), (1000, 32), jnp.float32)
        tbl_18 = 0.05 * jax.random.normal(jax.random.fold_in(_tk, 500 + 18), (1250, 32), jnp.float32)
        tbl_19 = 0.05 * jax.random.normal(jax.random.fold_in(_tk, 500 + 19), (1250, 32), jnp.float32)
        tbl_20 = 0.05 * jax.random.normal(jax.random.fold_in(_tk, 500 + 20), (1250, 32), jnp.float32)
        tbl_21 = 0.05 * jax.random.normal(jax.random.fold_in(_tk, 500 + 21), (1000, 32), jnp.float32)
        tbl_22 = 0.05 * jax.random.normal(jax.random.fold_in(_tk, 500 + 22), (12500, 32), jnp.float32)
        tbl_23 = 0.05 * jax.random.normal(jax.random.fold_in(_tk, 500 + 23), (125000, 32), jnp.float32)
        tbl_24 = 0.05 * jax.random.normal(jax.random.fold_in(_tk, 500 + 24), (1000, 32), jnp.float32)
        tbl_25 = 0.05 * jax.random.normal(jax.random.fold_in(_tk, 500 + 25), (12500, 32), jnp.float32)
        tbl_26 = 0.05 * jax.random.normal(jax.random.fold_in(_tk, 500 + 26), (1000, 32), jnp.float32)
        tbl_27 = 0.05 * jax.random.normal(jax.random.fold_in(_tk, 500 + 27), (125000, 32), jnp.float32)
        tbl_28 = 0.05 * jax.random.normal(jax.random.fold_in(_tk, 500 + 28), (1000, 32), jnp.float32)
        tbl_29 = 0.05 * jax.random.normal(jax.random.fold_in(_tk, 500 + 29), (1000, 32), jnp.float32)
        tbl_30 = 0.05 * jax.random.normal(jax.random.fold_in(_tk, 500 + 30), (1250, 32), jnp.float32)
        tbl_31 = 0.05 * jax.random.normal(jax.random.fold_in(_tk, 500 + 31), (12500, 32), jnp.float32)
        tbl_32 = 0.05 * jax.random.normal(jax.random.fold_in(_tk, 500 + 32), (12500, 32), jnp.float32)
        tbl_33 = 0.05 * jax.random.normal(jax.random.fold_in(_tk, 500 + 33), (12500, 32), jnp.float32)
        tbl_34 = 0.05 * jax.random.normal(jax.random.fold_in(_tk, 500 + 34), (1250, 32), jnp.float32)
        tbl_35 = 0.05 * jax.random.normal(jax.random.fold_in(_tk, 500 + 35), (12500, 32), jnp.float32)
        tbl_36 = 0.05 * jax.random.normal(jax.random.fold_in(_tk, 500 + 36), (12500, 32), jnp.float32)
        tbl_37 = 0.05 * jax.random.normal(jax.random.fold_in(_tk, 500 + 37), (1000, 32), jnp.float32)
        tbl_38 = 0.05 * jax.random.normal(jax.random.fold_in(_tk, 500 + 38), (1250, 32), jnp.float32)
        tbl_39 = 0.05 * jax.random.normal(jax.random.fold_in(_tk, 500 + 39), (12500, 32), jnp.float32)
        tbl_40 = 0.05 * jax.random.normal(jax.random.fold_in(_tk, 500 + 40), (1250, 32), jnp.float32)
        tbl_41 = 0.05 * jax.random.normal(jax.random.fold_in(_tk, 500 + 41), (1250, 32), jnp.float32)
        tbl_42 = 0.05 * jax.random.normal(jax.random.fold_in(_tk, 500 + 42), (1250, 32), jnp.float32)
        tbl_43 = 0.05 * jax.random.normal(jax.random.fold_in(_tk, 500 + 43), (1000, 32), jnp.float32)
        tbl_44 = 0.05 * jax.random.normal(jax.random.fold_in(_tk, 500 + 44), (1250, 32), jnp.float32)
        tbl_45 = 0.05 * jax.random.normal(jax.random.fold_in(_tk, 500 + 45), (12500, 32), jnp.float32)
        tbl_46 = 0.05 * jax.random.normal(jax.random.fold_in(_tk, 500 + 46), (12500, 32), jnp.float32)
        tbl_47 = 0.05 * jax.random.normal(jax.random.fold_in(_tk, 500 + 47), (1250, 32), jnp.float32)
        _rk = jax.random.fold_in(_tk, 7)
        W_top1 = 0.0693375 * jax.random.normal(jax.random.fold_in(_tk, 801), (208, 512), jnp.float32)
        W_top2 = 0.0441942 * jax.random.normal(jax.random.fold_in(_tk, 802), (512, 256), jnp.float32)
        W_top3 = 0.0625 * jax.random.normal(jax.random.fold_in(_tk, 803), (256, 1), jnp.float32)
        b_top1 = jnp.zeros((512,), jnp.float32)
        b_top2 = jnp.zeros((256,), jnp.float32)
        return (dense_ctx, ids, tbl_0, tbl_1, tbl_2, tbl_3, tbl_4, tbl_5, tbl_6, tbl_7, tbl_8, tbl_9, tbl_10, tbl_11, tbl_12, tbl_13, tbl_14, tbl_15, tbl_16, tbl_17, tbl_18, tbl_19, tbl_20, tbl_21, tbl_22, tbl_23, tbl_24, tbl_25, tbl_26, tbl_27, tbl_28, tbl_29, tbl_30, tbl_31, tbl_32, tbl_33, tbl_34, tbl_35, tbl_36, tbl_37, tbl_38, tbl_39, tbl_40, tbl_41, tbl_42, tbl_43, tbl_44, tbl_45, tbl_46, tbl_47, W_top1, b_top1, W_top2, b_top2, W_top3)
    dense_ctx, ids, tbl_0, tbl_1, tbl_2, tbl_3, tbl_4, tbl_5, tbl_6, tbl_7, tbl_8, tbl_9, tbl_10, tbl_11, tbl_12, tbl_13, tbl_14, tbl_15, tbl_16, tbl_17, tbl_18, tbl_19, tbl_20, tbl_21, tbl_22, tbl_23, tbl_24, tbl_25, tbl_26, tbl_27, tbl_28, tbl_29, tbl_30, tbl_31, tbl_32, tbl_33, tbl_34, tbl_35, tbl_36, tbl_37, tbl_38, tbl_39, tbl_40, tbl_41, tbl_42, tbl_43, tbl_44, tbl_45, tbl_46, tbl_47, W_top1, b_top1, W_top2, b_top2, W_top3 = _rec_inputs()

    def _L0_rec_setup():
        import jax, jax.numpy as jnp
        import numpy as np
        B, F, K, C = (256, 48, 32, 128)
        key = jax.random.key(seed)
        k0, k1, k2 = jax.random.split(key, 3)
        x = jax.random.normal(k0, (B, F, K), dtype=jnp.float32)
        W0 = jax.random.normal(k1, (F * F, C), dtype=jnp.float32) * 0.02
        b0 = jnp.zeros((C,), dtype=jnp.float32)
        W1 = jax.random.normal(k2, (F * (C // 2), C), dtype=jnp.float32) * 0.02
        b1 = jnp.zeros((C,), dtype=jnp.float32)
        return {'x': x, 'W0': W0, 'b0': b0, 'W1': W1, 'b1': b1}
    _L0_rec_all = _L0_rec_setup()
    _L0_rec_in = {k: v for k, v in _L0_rec_all.items() if k in ('W0', 'b0', 'W1', 'b1')}
    del _L0_rec_all
    return {'dense_ctx': dense_ctx, 'ids': ids, 'tbl_0': tbl_0, 'tbl_1': tbl_1, 'tbl_2': tbl_2, 'tbl_3': tbl_3, 'tbl_4': tbl_4, 'tbl_5': tbl_5, 'tbl_6': tbl_6, 'tbl_7': tbl_7, 'tbl_8': tbl_8, 'tbl_9': tbl_9, 'tbl_10': tbl_10, 'tbl_11': tbl_11, 'tbl_12': tbl_12, 'tbl_13': tbl_13, 'tbl_14': tbl_14, 'tbl_15': tbl_15, 'tbl_16': tbl_16, 'tbl_17': tbl_17, 'tbl_18': tbl_18, 'tbl_19': tbl_19, 'tbl_20': tbl_20, 'tbl_21': tbl_21, 'tbl_22': tbl_22, 'tbl_23': tbl_23, 'tbl_24': tbl_24, 'tbl_25': tbl_25, 'tbl_26': tbl_26, 'tbl_27': tbl_27, 'tbl_28': tbl_28, 'tbl_29': tbl_29, 'tbl_30': tbl_30, 'tbl_31': tbl_31, 'tbl_32': tbl_32, 'tbl_33': tbl_33, 'tbl_34': tbl_34, 'tbl_35': tbl_35, 'tbl_36': tbl_36, 'tbl_37': tbl_37, 'tbl_38': tbl_38, 'tbl_39': tbl_39, 'tbl_40': tbl_40, 'tbl_41': tbl_41, 'tbl_42': tbl_42, 'tbl_43': tbl_43, 'tbl_44': tbl_44, 'tbl_45': tbl_45, 'tbl_46': tbl_46, 'tbl_47': tbl_47, 'W_top1': W_top1, 'b_top1': b_top1, 'W_top2': W_top2, 'b_top2': b_top2, 'W_top3': W_top3, 'L0_rec_W0': _L0_rec_in['W0'], 'L0_rec_b0': _L0_rec_in['b0'], 'L0_rec_W1': _L0_rec_in['W1'], 'L0_rec_b1': _L0_rec_in['b1']}

def reference(dense_ctx, ids, tbl_0, tbl_1, tbl_2, tbl_3, tbl_4, tbl_5, tbl_6, tbl_7, tbl_8, tbl_9, tbl_10, tbl_11, tbl_12, tbl_13, tbl_14, tbl_15, tbl_16, tbl_17, tbl_18, tbl_19, tbl_20, tbl_21, tbl_22, tbl_23, tbl_24, tbl_25, tbl_26, tbl_27, tbl_28, tbl_29, tbl_30, tbl_31, tbl_32, tbl_33, tbl_34, tbl_35, tbl_36, tbl_37, tbl_38, tbl_39, tbl_40, tbl_41, tbl_42, tbl_43, tbl_44, tbl_45, tbl_46, tbl_47, W_top1, b_top1, W_top2, b_top2, W_top3, L0_rec_W0, L0_rec_b0, L0_rec_W1, L0_rec_b1):
    import jax
    import jax.numpy as jnp

    def _L0_rec_ref(x, W0, b0, W1, b1):
        import jax, jax.numpy as jnp
        import numpy as np
        B, F, K, C = (256, 48, 32, 128)
        x0 = jnp.transpose(x, (0, 2, 1))
        xk = x0
        results = []
        for i, (W, b) in enumerate(((W0, b0), (W1, b1))):
            fv = xk.shape[2]
            cross = jnp.einsum('bkf,bkg->bkfg', x0, xk).reshape(x.shape[0], K, F * fv)
            z = jax.nn.relu(jnp.einsum('bkc,cd->bkd', cross, W) + b)
            if i != 1:
                xk, direct = jnp.split(z, 2, axis=2)
            else:
                direct = z
            results.append(direct)
        out = jnp.concatenate(results, axis=2).sum(axis=1)
        return out
    e = jnp.stack([tbl_0[ids[:, 0]], tbl_1[ids[:, 1]], tbl_2[ids[:, 2]], tbl_3[ids[:, 3]], tbl_4[ids[:, 4]], tbl_5[ids[:, 5]], tbl_6[ids[:, 6]], tbl_7[ids[:, 7]], tbl_8[ids[:, 8]], tbl_9[ids[:, 9]], tbl_10[ids[:, 10]], tbl_11[ids[:, 11]], tbl_12[ids[:, 12]], tbl_13[ids[:, 13]], tbl_14[ids[:, 14]], tbl_15[ids[:, 15]], tbl_16[ids[:, 16]], tbl_17[ids[:, 17]], tbl_18[ids[:, 18]], tbl_19[ids[:, 19]], tbl_20[ids[:, 20]], tbl_21[ids[:, 21]], tbl_22[ids[:, 22]], tbl_23[ids[:, 23]], tbl_24[ids[:, 24]], tbl_25[ids[:, 25]], tbl_26[ids[:, 26]], tbl_27[ids[:, 27]], tbl_28[ids[:, 28]], tbl_29[ids[:, 29]], tbl_30[ids[:, 30]], tbl_31[ids[:, 31]], tbl_32[ids[:, 32]], tbl_33[ids[:, 33]], tbl_34[ids[:, 34]], tbl_35[ids[:, 35]], tbl_36[ids[:, 36]], tbl_37[ids[:, 37]], tbl_38[ids[:, 38]], tbl_39[ids[:, 39]], tbl_40[ids[:, 40]], tbl_41[ids[:, 41]], tbl_42[ids[:, 42]], tbl_43[ids[:, 43]], tbl_44[ids[:, 44]], tbl_45[ids[:, 45]], tbl_46[ids[:, 46]], tbl_47[ids[:, 47]]], axis=1)
    z = _L0_rec_ref(e, L0_rec_W0, L0_rec_b0, L0_rec_W1, L0_rec_b1)
    z = z.reshape(z.shape[0], -1)
    h = jnp.concatenate([z, dense_ctx], axis=1)
    h = jnp.maximum(h @ W_top1 + b_top1, 0.0)
    h = jnp.maximum(h @ W_top2 + b_top2, 0.0)
    y = h @ W_top3
    return y

_drawn_inputs = setup_inputs


def setup_inputs(seed=0):
    import zlib

    import numpy as np

    out = dict(_drawn_inputs(seed))
    spreads = {'b_top1': (0.0, 2.0),
     'b_top2': (0.0, 0.749),
     'L0_rec_b0': (0.0, 0.1),
     'L0_rec_b1': (0.0, 0.319)}
    factors = {'tbl_0': 8.0,
     'tbl_1': 8.0,
     'tbl_2': 8.0,
     'tbl_3': 8.0,
     'tbl_4': 8.0,
     'tbl_5': 8.0,
     'tbl_6': 8.0,
     'tbl_7': 8.0,
     'tbl_8': 8.0,
     'tbl_9': 8.0,
     'tbl_10': 8.0,
     'tbl_11': 8.0,
     'tbl_12': 8.0,
     'tbl_13': 8.0,
     'tbl_14': 8.0,
     'tbl_15': 8.0,
     'tbl_16': 8.0,
     'tbl_17': 8.0,
     'tbl_18': 8.0,
     'tbl_19': 8.0,
     'tbl_20': 8.0,
     'tbl_21': 8.0,
     'tbl_22': 8.0,
     'tbl_23': 8.0,
     'tbl_24': 8.0,
     'tbl_25': 8.0,
     'tbl_26': 8.0,
     'tbl_27': 8.0,
     'tbl_28': 8.0,
     'tbl_29': 8.0,
     'tbl_30': 8.0,
     'tbl_31': 8.0,
     'tbl_32': 8.0,
     'tbl_33': 8.0,
     'tbl_34': 8.0,
     'tbl_35': 8.0,
     'tbl_36': 8.0,
     'tbl_37': 8.0,
     'tbl_38': 8.0,
     'tbl_39': 8.0,
     'tbl_40': 8.0,
     'tbl_41': 8.0,
     'tbl_42': 8.0,
     'tbl_43': 8.0,
     'tbl_44': 8.0,
     'tbl_45': 8.0,
     'tbl_46': 8.0,
     'tbl_47': 8.0,
     'L0_rec_W0': 7.539,
     'L0_rec_W1': 4.924,
     'dense_ctx': 4.539}
    for name, (base, spread) in spreads.items():
        noise = np.random.default_rng([zlib.crc32(name.encode()), seed]).standard_normal(out[name].shape)
        drawn = base * np.exp(spread * noise) if base else spread * noise
        out[name] = jnp.asarray(drawn.astype(out[name].dtype))
    for name, factor in factors.items():
        out[name] = (out[name] * factor).astype(out[name].dtype)
    return out
```

```python
import numpy as np
from contextlib import ExitStack

import concourse.bass as bass
from concourse import mybir

F32 = mybir.dt.float32
F32R = mybir.dt.float32r
I32 = mybir.dt.int32
ALU = mybir.AluOpType
ACT = mybir.ActivationFunctionType
AX = mybir.AxisListType

B, F, K, C = 512, 48, 32, 128
HID = C // 2
DENSE = 16
N1, N2 = 512, 256
P = 128
NBLK = B // P
KT = 4
COLS = KT * P
TILES = B * K // COLS
U, V = 8, 16
NA = F // U
NBX, NBY = F // V, HID // V

PAIRS = [(0, b, i) for b in range(NBX) for i in range(b + 1)] + \
        [(1, b, i) for b in range(NBY) for i in range(NA // 2)]
NP = len(PAIRS)
NP0 = sum(1 for p in PAIRS if p[0] == 0)
NP1 = NP - NP0
GROUP = [b if l == 0 else NBX + b for l, b, i in PAIRS]
NG = NBX + NBY
FIRST = [GROUP.index(g) for g in range(NG)]
LAST = [NP - 1 - GROUP[::-1].index(g) for g in range(NG)]
KIND = "PDPNPDPDPNPDPDPNPD"
assert len(KIND) == NP
SPLIT = [j for j in range(NP) if KIND[j] != "N"]
NATIVE = [j for j in range(NP) if KIND[j] == "N"]
RING = NP0
assert NP0 % RING == 0 and NP1 % RING == 0
LEAD = 5
GATHERS_PER_STEP = 7
LOOP_FROM = 5
assert LOOP_FROM % 2 == 1 and TILES % 2 == 0


def pair_index(s, j):
    if isinstance(s, int):
        if s == 0:
            return j
        if s == TILES:
            return NP * s - NP1 + j - NP0
    return s * NP + (j - NP1)


def count(kinds, s, j):
    n0 = sum(1 for x in range(NP0) if KIND[x] in kinds)
    n1 = sum(1 for x in range(NP0, NP) if KIND[x] in kinds)
    here = sum(1 for x in range(j + 1) if KIND[x] in kinds)
    if isinstance(s, int):
        if s == 0:
            return here
        if s == TILES:
            here -= n0
    return s * (n0 + n1) + (here - n1)


def group_index(s, g):
    if isinstance(s, int):
        if s == 0:
            return g
        if s == TILES:
            return NG * s - NBY + g - NBX
    return s * NG + (g - NBY)


def group_bank(s, par, g):
    if isinstance(s, int):
        return group_index(s, g) % 2
    return (par * NG + g - NBY) % 2


def present(s, j):
    if isinstance(s, int):
        return 0 <= s <= TILES and not (s == 0 and j >= NP0) and not (s == TILES and j < NP0)
    return True


def steps(engine, step):
    for s in range(-1, LOOP_FROM):
        step(s, s // 2, s % 2)
    with engine.Fori(0, (TILES - 1 - LOOP_FROM) // 2) as i:
        step(i * 2 + LOOP_FROM, i + LOOP_FROM // 2, 1)
        step(i * 2 + LOOP_FROM + 1, i + LOOP_FROM // 2 + 1, 0)
    for s in (TILES - 1, TILES):
        step(s, s // 2, s % 2)


def has(s, lo, hi):
    return not isinstance(s, int) or lo <= s <= hi


def build(nc, ids, dense, tables, w0, b0, w1, b1, wt1, bt1, wt2, bt2, wt3, out):
    with ExitStack() as ctx:
        def sb(name, shape, dt):
            return ctx.enter_context(nc.sbuf_tensor(name, shape, dt))

        def pb(name, shape, dt):
            return ctx.enter_context(nc.psum_tensor(name, shape, dt))

        def sem(name):
            return ctx.enter_context(nc.semaphore(name))

        idx = sb("idx", [P, NBLK, F], I32)
        rows = sb("rows", [P, F, NBLK * K], F32)
        rows_t = sb("rows_t", [P, KT, P], F32)
        ident = sb("ident", [P, P], F32)
        pick = sb("pick", [P, NA + NBY, P], F32R)
        xs = sb("xs", [P, COLS], F32R)
        left = sb("left", [P, 2, NA, COLS], F32)
        y = sb("y", [P, 2, COLS], F32)
        ys = sb("ys", [P, 2, COLS], F32R)
        z = sb("z", [P, 2, COLS], F32)
        prod = sb("prod", [P, RING, 2, COLS], F32)
        prod_hi = sb("prod_hi", [P, RING, 2, COLS], F32R)
        prod_lo = sb("prod_lo", [P, RING, 2, COLS], F32R)
        w_full = sb("w_full", [P, max(1, len(NATIVE)), 2, C], F32)
        w_hi = sb("w_hi", [P, len(SPLIT), 2, C], F32R)
        w_lo = sb("w_lo", [P, len(SPLIT), 2, C], F32R)
        sums0 = sb("sums0", [P, TILES // 2, P], F32)
        sums1 = sb("sums1", [P, TILES // 2, P], F32)
        bias0 = sb("bias0", [P, 1], F32)
        bias1 = sb("bias1", [P, 1], F32)
        top1 = sb("top1", [P, 2, N1], F32)
        top2 = sb("top2", [P, N1 // P, N2], F32)
        top3 = sb("top3", [P, N2 // P], F32)
        tbias1 = sb("tbias1", [P, N1 // P], F32)
        tbias2 = sb("tbias2", [P, N2 // P], F32)
        dense_in = sb("dense_in", [P, NBLK, DENSE], F32)
        h_in = sb("h_in", [P, 2, B], F32)
        h1 = left[:, 0, 0:N1 // P, :]
        h2 = left[:, 1, 0:N2 // P, :]
        y_out = z[0:1, 0, :]
        pick_f = sums1[:, 0:NA + NBY, :]
        w0_fg = prod[:, 0:3].rearrange("p r e c -> p (r e c)")[:, 0:NA * NBX * C] \
            .rearrange("p (a b c) -> p a b c", a=NA, b=NBX)
        w0_gf = prod[:, 3:6].rearrange("p r e c -> p (r e c)")[:, 0:NA * NBX * C] \
            .rearrange("p (a b c) -> p a b c", a=NA, b=NBX)
        w1_fh = left[:, 0].rearrange("p a c -> p (a c)").rearrange("p (a b c) -> p a b c", a=NA, b=NBY)

        def weight(j):
            layer, b, i = PAIRS[j]
            return (w0_fg, w1_fh)[layer][:, 2 * i:2 * i + 2, b, :]

        acc0 = pb("acc0", [P, COLS], F32)
        acc1 = pb("acc1", [P, COLS], F32)
        right = pb("right", [P, 2, COLS], F32)
        stage = pb("stage", [P, 2, COLS], F32)
        prod_ps = pb("prod_ps", [P, 2, COLS], F32)

        ids_in = sem("ids_in")
        gathered = [sem(f"gathered{m}") for m in range(NBLK)]
        w_in = sem("w_in")
        small_in = sem("small_in")
        dense_inn = sem("dense_inn")
        consts = sem("consts")
        picks = sem("picks")
        pad0 = sem("pad0")
        w_sum = sem("w_sum")
        w_his = sem("w_his")
        w_los = sem("w_los")
        dense_t = sem("dense_t")
        dense_c = sem("dense_c")
        zeroed = sem("zeroed")
        tile_in = sem("tile_in")
        rows_t_ready = sem("rows_t_ready")
        transposed = sem("transposed")
        x_hi = sem("x_hi")
        x_lo = sem("x_lo")
        left_made = sem("left_made")
        left_ready = sem("left_ready")
        right_ready = sem("right_ready")
        multiplied = sem("multiplied")
        hi_ready = sem("hi_ready")
        lo_by_dve = sem("lo_by_dve")
        lo_by_pool = sem("lo_by_pool")
        contracted = sem("contracted")
        y_ready = sem("y_ready")
        y_hi = sem("y_hi")
        y_lo = sem("y_lo")
        z_ready = sem("z_ready")
        summed0 = sem("summed0")
        summed1 = sem("summed1")
        h_ready = sem("h_ready")
        top_mm = sem("top_mm")
        top_act = sem("top_act")
        stored = sem("stored")

        block = ctx.enter_context(nc.Block())
        W_DMAS = U * (2 * NBX + NBY)

        def load_weight(engine, dst, src, u, b):
            engine.dma_start(dst[V * u:V * (u + 1), :, b, :], src[u, b]).then_inc(w_in, 16)

        @block.sync
        def _(sp):
            sp.dma_start(idx[:], ids.rearrange("(m p) f -> p m f", p=P)).then_inc(ids_in, 16)
            for u in range(U):
                for b in range(NBX):
                    load_weight(sp, w0_fg, w0.rearrange("(a u b v) c -> u b v a c", a=NA, u=U, b=NBX), u, b)
                    load_weight(sp, w0_gf, w0.rearrange("(b v a u) c -> u b v a c", b=NBX, v=V, a=NA), u, b)
            sp.dma_start(bias0[:], b0.rearrange("(p o) -> p o", o=1)).then_inc(small_in, 16)
            sp.dma_start(bias1[:], b1.rearrange("(p o) -> p o", o=1)).then_inc(small_in, 16)
            sp.dma_start(tbias1[:], bt1.rearrange("(p n) -> p n", p=P)).then_inc(small_in, 16)
            sp.dma_start(tbias2[:], bt2.rearrange("(p n) -> p n", p=P)).then_inc(small_in, 16)
            sp.dma_start(top3[:], wt3.rearrange("(p n) o -> p (n o)", p=P)).then_inc(small_in, 16)
            sp.dma_start(top2[:], wt2.rearrange("(p n) c -> p n c", p=P)).then_inc(small_in, 16)
            sp.dma_start(top1[:, 1, :], wt1[HID:HID + P, :]).then_inc(small_in, 16)
            sp.dma_start(dense_in[:], dense.rearrange("(m p) d -> p m d", p=P)).then_inc(dense_inn, 16)
            sp.wait_ge(zeroed, 1)
            sp.dma_start(top1[HID:P, 0, :], wt1[0:HID, :]).then_inc(small_in, 16)
            sp.dma_start(top1[0:DENSE, 0, :], wt1[HID + P:HID + P + DENSE, :]).then_inc(small_in, 16)
            sp.wait_ge(top_act, 3)
            sp.dma_start(out.rearrange("b o -> o b"), y_out).then_inc(stored, 16)
            sp.wait_ge(stored, 16)

        @block.gpsimd
        def _(pool):
            def gather(m, f):
                nc.gpsimd.indirect_dma_start(
                    rows[:, f, m * K:(m + 1) * K], None, tables[f],
                    bass.IndirectOffsetOnAxis(ap=idx[:, m, f:f + 1], axis=0)).then_inc(gathered[m], 16)

            pool.wait_ge(ids_in, 16)
            for f in range(F // 2):
                gather(0, f)
            nc.gpsimd.memset(ident[:], 0.0).then_inc(consts, 1)
            nc.gpsimd.memset(pick_f[:], 0.0).then_inc(consts, 1)
            pool.wait_ge(consts, 2)
            nc.gpsimd.affine_select(out=ident[:], in_=ident[:], compare_op=ALU.not_equal, fill=1.0, base=0,
                                    pattern=[[-1, P]], channel_multiplier=1).then_inc(consts, 1)
            lefts = pick_f[:, 0:NA, :].rearrange("p a (u v) -> p a u v", u=U)
            rights = pick_f[:, NA:NA + NBY, :].rearrange("p b (u v) -> p b u v", u=U)
            n = 3
            for base in (0, -HID):
                nc.gpsimd.affine_select(out=lefts, in_=lefts, compare_op=ALU.not_equal, fill=1.0, base=base,
                                        pattern=[[-U, NA], [-1, U], [0, V]], channel_multiplier=1) \
                    .then_inc(consts, 1)
                nc.gpsimd.affine_select(out=rights, in_=rights, compare_op=ALU.not_equal, fill=1.0, base=base,
                                        pattern=[[-V, NBY], [0, U], [-1, V]], channel_multiplier=1) \
                    .then_inc(consts, 1)
                n += 2
                pool.wait_ge(consts, n)
            for f in range(F // 2, F):
                gather(0, f)

            def step(s, gathers=()):
                pairs = [j for j in range(NP) if KIND[j] == "P" and present(s, j)]
                gathers = list(gathers)
                for j in pairs:
                    for m, f in gathers[:1]:
                        gather(m, f)
                    gathers = gathers[1:]
                    pool.wait_ge(hi_ready, count("DP", s, j))
                    nc.gpsimd.tensor_tensor(prod_lo[:, j % RING], prod[:, j % RING],
                                            prod_hi[:, j % RING].bitcast(F32), ALU.subtract) \
                        .then_inc(lo_by_pool, 1)
                for m, f in gathers:
                    gather(m, f)

            def admit():
                pool.sem_inc(tile_in, 1)

            pool.wait_ge(gathered[0], 16 * F)
            for t in range(P // (KT * NBLK)):
                admit()
            tiles_per_block = TILES // NBLK
            queue = [(m, f) for m in range(1, NBLK) for f in range(F)]
            last_gather_step = (NBLK - 1) * tiles_per_block
            for s in range(last_gather_step):
                m = s // tiles_per_block + 1
                mine = [q for q in queue if q[0] == m][:GATHERS_PER_STEP]
                queue = [q for q in queue if q not in mine]
                step(s, mine)
                if s % tiles_per_block == tiles_per_block - 2:
                    pool.wait_ge(gathered[m], 16 * F)
                    for t in range(tiles_per_block):
                        admit()
            assert not queue
            with pool.Fori(last_gather_step, TILES) as s:
                step(s)
            step(TILES)

        @block.tensor
        def _(pe):
            pe.wait_ge(consts, 3)
            pe.wait_ge(dense_inn, 16)
            for m in range(NBLK):
                last = nc.tensor.transpose(acc0[0:DENSE, m * P:(m + 1) * P], dense_in[:, m, :], ident[:])
            last.then_inc(dense_t, 1)
            pe.wait_ge(picks, 1)
            pe.wait_ge(w_his, 1)
            pe.wait_ge(w_los, 1)
            pe.wait_ge(dense_c, 1)

            def transpose(t, par):
                pe.wait_ge(rows_t_ready, t + 1)
                if has(t, 1, TILES):
                    pe.wait_ge(left_ready, t * NA - 1)
                for k in range(KT):
                    last = nc.tensor.transpose(stage[:, par, k * P:(k + 1) * P], rows_t[:, k, :], ident[:])
                last.then_inc(transposed, 1)

            def make_left(t, par, a):
                if a == 0:
                    pe.wait_ge(x_hi, t + 1)
                    pe.wait_ge(x_lo, t + 1)
                if a >= 2 or (a == 0 and has(t, 1, TILES)):
                    pe.wait_ge(left_ready, t * NA + a - (0 if a == 0 else 1))
                nc.tensor.matmul(stage[:, (par + 1 + a) % 2, :], pick[:, a, :], xs[:], start=True, stop=True) \
                    .then_inc(left_made, 1)

            def make_right(s, par, g):
                n = group_index(s, g)
                if not isinstance(n, int) or n >= 2:
                    if g >= 2:
                        done = pair_index(s, LAST[g - 2]) + 1
                        if isinstance(s, int) and s == TILES and g - 2 < NBX:
                            done = pair_index(s - 1, LAST[NG - 2 + (g - NBX)]) + 1
                    else:
                        done = pair_index(s - 1, LAST[g - 2 + NG]) + 1
                    if isinstance(s, int) and s == 1 and g < 2:
                        done = LAST[NBX - 2 + g] + 1
                    pe.wait_ge(multiplied, done)
                if g == NBX:
                    pe.wait_ge(y_hi, s)
                    pe.wait_ge(y_lo, s)
                src = xs[:] if g < NBX else ys[:, (par + 1) % 2, :]
                b = g if g < NBX else g - NBX
                nc.tensor.matmul(right[:, group_bank(s, par, g), :], pick[:, NA + b, :], src,
                                 start=True, stop=True).then_inc(right_ready, 1)

            def contract(s, j):
                layer = PAIRS[j][0]
                acc = (acc0, acc1)[layer][:]
                lo_j, hi_j = (0, NP0 - 1) if layer == 0 else (NP0, NP - 1)
                if j == 0 and has(s, 1, TILES):
                    pe.wait_ge(y_hi, s)
                if j == NP0 and has(s, 2, TILES):
                    pe.wait_ge(z_ready, s - 1)
                slot = j % RING
                if KIND[j] == "N":
                    pe.wait_ge(multiplied, pair_index(s, j) + 1)
                    n = NATIVE.index(j)
                    for e in range(2):
                        last = nc.tensor.matmul(acc, w_full[:, n, e, :], prod[:, slot, e, :],
                                                start=(j == lo_j and e == 0), stop=(j == hi_j and e == 1))
                else:
                    n = SPLIT.index(j)
                    pe.wait_ge(hi_ready, count("DP", s, j))
                    for e in range(2):
                        nc.tensor.matmul(acc, w_hi[:, n, e, :], prod_hi[:, slot, e, :],
                                         start=(j == lo_j and e == 0), stop=False)
                        nc.tensor.matmul(acc, w_lo[:, n, e, :], prod_hi[:, slot, e, :], start=False, stop=False)
                    if KIND[j] == "D":
                        pe.wait_ge(lo_by_dve, count("D", s, j))
                    else:
                        pe.wait_ge(lo_by_pool, count("P", s, j))
                    for e in range(2):
                        last = nc.tensor.matmul(acc, w_hi[:, n, e, :], prod_lo[:, slot, e, :],
                                                start=False, stop=(j == hi_j and e == 1))
                last.then_inc(contracted, 1)

            AT_TRANSPOSE = 7
            AT_LEFT = [11, 11, 13, 13, 15, 15]

            def step(s, half, par):
                for j in range(NP):
                    if has(s, -1, TILES - 2 + 1 - 0) and (not isinstance(s, int) or s + 1 < TILES):
                        if j == AT_TRANSPOSE:
                            transpose(s + 1, 1 - par)
                        for a in range(NA):
                            if AT_LEFT[a] == j:
                                make_left(s + 1, 1 - par, a)
                    for g in range(NG):
                        at = FIRST[g] - LEAD
                        if at < 0 and at + NP == j and (not isinstance(s, int) or -1 <= s < TILES - 1):
                            if g < NBX:
                                make_right(s + 1, 1 - par, g)
                        if at == j and g >= NBX and has(s, 1, TILES):
                            make_right(s, par, g)
                    if present(s, j):
                        contract(s, j)

            steps(pe, step)

            pe.wait_ge(small_in, 16 * 9)
            pe.wait_ge(h_ready, 3)
            banks = [acc0[:], acc1[:], stage[:, 0, :], stage[:, 1, :]]
            for n in range(N1 // P):
                for c in range(2):
                    last = nc.tensor.matmul(banks[n], top1[:, c, :].rearrange("p (m n) -> p n m", m=P)[:, n, :], h_in[:, c, :],
                                            start=(c == 0), stop=(c == 1))
            last.then_inc(top_mm, 1)
            pe.wait_ge(top_act, 1)
            for n in range(N2 // P):
                for c in range(N1 // P):
                    last = nc.tensor.matmul(right[:, n, :], top2[:, c, :].rearrange("p (m n) -> p n m", m=P)[:, n, :], h1[:, c, :],
                                            start=(c == 0), stop=(c == N1 // P - 1))
            last.then_inc(top_mm, 1)
            pe.wait_ge(top_act, 2)
            for c in range(N2 // P):
                last = nc.tensor.matmul(prod_ps[0:1, 0, :], top3[:, c:c + 1], h2[:, c, :],
                                        start=(c == 0), stop=(c == N2 // P - 1))
            last.then_inc(top_mm, 1)

        @block.vector
        def _(dve):
            nc.vector.memset(rows_t[:], 0.0).then_inc(pad0, 1)
            nc.vector.memset(top1[:, 0, :], 0.0)
            nc.vector.memset(h_in[:, 0, :], 0.0).then_inc(zeroed, 1)
            dve.wait_ge(consts, 7)
            nc.vector.tensor_copy(pick[:], pick_f[:]).then_inc(picks, 1)
            dve.wait_ge(zeroed, 1)
            dve.wait_ge(dense_t, 1)
            nc.vector.tensor_copy(h_in[0:DENSE, 0, :], acc0[0:DENSE, :]).then_inc(dense_c, 1)
            dve.wait_ge(w_in, 16 * W_DMAS)
            for b in range(1, NBX):
                last = nc.vector.tensor_tensor(w0_fg[:, 0:2 * b, b, :], w0_fg[:, 0:2 * b, b, :],
                                               w0_gf[:, 0:2 * b, b, :], ALU.add)
            last.then_inc(w_sum, 1)
            dve.wait_ge(w_his, 1)
            for n, j in enumerate(SPLIT):
                last = nc.vector.tensor_tensor(w_lo[:, n], weight(j), w_hi[:, n].bitcast(F32), ALU.subtract)
            last.then_inc(w_los, 1)

            def low_x(t, par):
                dve.wait_ge(x_hi, t + 1)
                nc.vector.tensor_tensor(xs[HID:P, :], stage[0:HID, par, :], xs[0:HID, :].bitcast(F32),
                                        ALU.subtract).then_inc(x_lo, 1)

            def low_y(s, par):
                dve.wait_ge(y_hi, s + 1)
                nc.vector.tensor_tensor(ys[HID:P, par, :], y[0:HID, par, :], ys[0:HID, par, :].bitcast(F32),
                                        ALU.subtract).then_inc(y_lo, 1)

            def multiply(s, par, j):
                layer, b, i = PAIRS[j]
                g = GROUP[j]
                q = pair_index(s, j)
                if j == FIRST[g]:
                    dve.wait_ge(right_ready, group_index(s, g) + 1)
                if layer == 0 and i == b:
                    dve.wait_ge(left_ready, s * NA + 2 * i + 2)
                if not isinstance(q, int) or q >= RING:
                    dve.wait_ge(contracted, q - RING + 1)
                t_par = par if layer == 0 else 1 - par
                dst = prod[:, j % RING]
                if KIND[j] == "D":
                    dst = prod_ps[:]
                    n = count("D", s, j)
                    if not isinstance(n, int) or n >= 2:
                        dve.wait_ge(lo_by_dve, n - 1)
                nc.vector.tensor_tensor(dst, right[:, group_bank(s, par, g), :].unsqueeze(1)
                                        .broadcast_to([P, 2, COLS]), left[:, t_par, 2 * i:2 * i + 2, :],
                                        ALU.mult).then_inc(multiplied, 1)

            def low(s, j):
                dve.wait_ge(hi_ready, count("DP", s, j))
                nc.vector.tensor_tensor(prod_lo[:, j % RING], prod_ps[:],
                                        prod_hi[:, j % RING].bitcast(F32), ALU.subtract).then_inc(lo_by_dve, 1)

            def sum_over_k(src, dst):
                return nc.vector.tensor_reduce(dst, src.rearrange("p t (k b) -> p b (t k)", k=KT), AX.X, ALU.add)

            def sum0(s, half):
                dve.wait_ge(y_ready, s)
                sum_over_k(y[HID:P], sums0[HID:P, bass.ds(half - 1, 1), :].rearrange("p o b -> p (o b)")) \
                    .then_inc(summed0, 1)

            def sum1(s, half):
                dve.wait_ge(z_ready, s - 1)
                sum_over_k(z[:], sums1[:, bass.ds(half - 1, 1), :].rearrange("p o b -> p (o b)")) \
                    .then_inc(summed1, 1)

            def step(s, half, par):
                late = None
                if par == 0 and has(s, 2, TILES):
                    sum0(s, half)
                for j in range(NP):
                    if present(s, j):
                        if late is not None and KIND[j] == "D":
                            low(s, late)
                            late = None
                        multiply(s, par, j)
                        if late is not None:
                            low(s, late)
                            late = None
                        if KIND[j] == "D":
                            late = j
                    elif late is not None:
                        low(s, late)
                        late = None
                    if j == 7 and par == 1 and has(s, 3, TILES):
                        sum1(s, half)
                    if j == 12 and has(s, 0, TILES - 1):
                        low_y(s, par)
                    if j == 13 and has(s, -1, TILES - 2):
                        low_x(s + 1, 1 - par)
                if late is not None:
                    low(s, late)

            steps(dve, step)

            sum1(TILES + 1, TILES // 2)
            dve.wait_ge(summed0, TILES // 2)
            dve.wait_ge(summed1, TILES // 2)
            dve.wait_ge(dense_c, 1)
            per = TILES // 2 // NBLK
            nc.vector.tensor_reduce(h_in[HID:P, 0, :].rearrange("p (m b) -> p m b", m=NBLK),
                                    sums0[HID:P].rearrange("p (m t) b -> p m b t", t=per),
                                    AX.X, ALU.add).then_inc(h_ready, 1)
            nc.vector.tensor_reduce(h_in[:, 1, :].rearrange("p (m b) -> p m b", m=NBLK),
                                    sums1[:].rearrange("p (m t) b -> p m b t", t=per),
                                    AX.X, ALU.add).then_inc(h_ready, 2)

        @block.scalar
        def _(act):
            for u in range(U):
                for b in range(NBY):
                    load_weight(act, w1_fh, w1.rearrange("(a u b v) c -> u b v a c", a=NA, u=U, b=NBY), u, b)
            act.wait_ge(w_sum, 1)
            for j in range(NP):
                if j in NATIVE:
                    last = nc.scalar.copy(w_full[:, NATIVE.index(j)], weight(j))
                else:
                    last = nc.scalar.copy(w_hi[:, SPLIT.index(j)], weight(j))
            last.then_inc(w_his, 1)
            act.wait_ge(pad0, 1)
            act.wait_ge(small_in, 16 * 9)
            act.wait_ge(w_los, 1)

            def take_rows(t):
                act.wait_ge(tile_in, t + 1)
                if has(t, 1, TILES):
                    act.wait_ge(transposed, t)
                nc.scalar.copy(rows_t[:, :, 0:F],
                               rows[:, :, bass.ds(t * KT, KT)].rearrange("p f k -> p k f")) \
                    .then_inc(rows_t_ready, 1)

            def high_x(t, par):
                act.wait_ge(transposed, t + 1)
                if has(t, 1, TILES):
                    act.wait_ge(right_ready, group_index(t - 1, NBX - 1) + 1)
                nc.scalar.copy(xs[0:HID, :], stage[0:HID, par, :]).then_inc(x_hi, 1)

            def store_left(t, par, a):
                act.wait_ge(left_made, t * NA + a + 1)
                if a % 2 == 0 and has(t, 2, TILES):
                    act.wait_ge(multiplied, pair_index(t - 1, NP - NA // 2 + a // 2) + 1)
                nc.scalar.copy(left[:, par, a, :], stage[:, (par + 1 + a) % 2, :]).then_inc(left_ready, 1)

            def high(s, j):
                act.wait_ge(multiplied, pair_index(s, j) + 1)
                src = prod_ps[:] if KIND[j] == "D" else prod[:, j % RING]
                nc.scalar.copy(prod_hi[:, j % RING], src).then_inc(hi_ready, 1)

            def relu0(s, half, par):
                act.wait_ge(contracted, pair_index(s, NP0 - 1) + 1)
                if has(s, 2, TILES):
                    act.wait_ge(summed0, half)
                    act.wait_ge(right_ready, group_index(s - 1, NG - 1) + 1)
                    act.wait_ge(y_lo, s - 1)
                nc.scalar.activation(y[:, par, :], acc0[:], ACT.Relu, bias=bias0[:]).then_inc(y_ready, 1)
                nc.scalar.activation(ys[0:HID, par, :], acc0[0:HID, :], ACT.Relu, bias=bias0[0:HID]) \
                    .then_inc(y_hi, 1)

            def relu1(s, half, par):
                act.wait_ge(contracted, pair_index(s - 1, NP - 1) + 1)
                if has(s, 4, TILES + 1):
                    act.wait_ge(summed1, half - 1)
                nc.scalar.activation(z[:, par, :], acc1[:], ACT.Relu, bias=bias1[:]).then_inc(z_ready, 1)

            def step(s, half, par):
                for j in range(NP):
                    if KIND[j] != "N" and present(s, j):
                        high(s, j)
                    if j == 5 and has(s, 2, TILES):
                        relu1(s, half, par)
                    if j == 8 and has(s, -1, TILES - 2):
                        take_rows(s + 1)
                    if j == 11 and has(s, 0, TILES - 1):
                        relu0(s, half, par)
                    if j == 13 and has(s, -1, TILES - 2):
                        high_x(s + 1, 1 - par)
                    if j >= 15 and has(s, -1, TILES - 2):
                        for a in (2 * (j - 15), 2 * (j - 15) + 1):
                            store_left(s + 1, 1 - par, a)

            steps(act, step)
            relu1(TILES + 1, (TILES + 1) // 2, (TILES + 1) % 2)

            banks = [acc0[:], acc1[:], stage[:, 0, :], stage[:, 1, :]]
            act.wait_ge(top_mm, 1)
            for n in range(N1 // P):
                last = nc.scalar.activation(h1[:, n, :], banks[n], ACT.Relu, bias=tbias1[:, n:n + 1])
            last.then_inc(top_act, 1)
            act.wait_ge(top_mm, 2)
            for n in range(N2 // P):
                last = nc.scalar.activation(h2[:, n, :], right[:, n, :], ACT.Relu, bias=tbias2[:, n:n + 1])
            last.then_inc(top_act, 1)
            act.wait_ge(top_mm, 3)
            nc.scalar.copy(y_out, prod_ps[0:1, 0, :]).then_inc(top_act, 1)


def kernel(**inputs):
    import concourse.bacc as bacc
    from concourse.bass_utils import run_bass_kernel_spmd

    nc = bacc.Bacc("TRN2", target_bir_lowering=False, num_devices=1)
    arrays = {}

    def put(name):
        a = np.ascontiguousarray(inputs[name])
        arrays["in_" + name] = a
        return nc.dram_tensor("in_" + name, a.shape, mybir.dt.from_np(a.dtype), kind="ExternalInput").ap()

    out = nc.dram_tensor("out_y", (B, 1), F32, kind="ExternalOutput").ap()
    tables = [put(f"tbl_{f}") for f in range(F)]
    build(nc, put("ids"), put("dense_ctx"), tables, put("L0_rec_W0"), put("L0_rec_b0"), put("L0_rec_W1"),
          put("L0_rec_b1"), put("W_top1"), put("b_top1"), put("W_top2"), put("b_top2"), put("W_top3"), out)
    r = run_bass_kernel_spmd(nc, [arrays], core_ids=[0])
    return r.results[0]["out_y"]
```

```python
import numpy as np
from contextlib import ExitStack

import concourse.bass as bass
from concourse import mybir

F32 = mybir.dt.float32
F32R = mybir.dt.float32r
I32 = mybir.dt.int32
ALU = mybir.AluOpType
ACT = mybir.ActivationFunctionType
AX = mybir.AxisListType

B, F, K, C = 512, 48, 32, 128
HID = C // 2
DENSE = 16
N1, N2 = 512, 256
P = 128
NBLK = B // P
KT = 4
COLS = KT * P
TILES = B * K // COLS
U, V = 8, 16
NA = F // U
NBX, NBY = F // V, HID // V
MIX = NA
SHIFTS = U // 2 + 1

RIGHT = [("x", 1), ("x", 2), ("x", 0), ("x", "mix"), ("y", 0), ("y", 1), ("y", 2), ("y", 3)]
NG, NGX, NGY = len(RIGHT), NBX + 1, NBY
BANKS = 4
assert NGX % BANKS == 0 and NGY % BANKS == 0
PAIRS0 = [((0, 0), (0, 1)), ((0, 1), (2, 3)), ((1, 1), (0, 1)), ((1, 1), (2, 4)), ((2, 3), (0, MIX))]
PAIRS1 = [((NGX + b, NGX + b), (2 * i, 2 * i + 1)) for b in range(NBY) for i in range(NA // 2)]
PAIRS = PAIRS0 + PAIRS1
NP0, NP1, NP = len(PAIRS0), len(PAIRS1), len(PAIRS)
FIRST = [min(j for j in range(NP) if g in PAIRS[j][0]) for g in range(NG)]
LAST = [max(j for j in range(NP) if g in PAIRS[j][0]) for g in range(NG)]
KIND = "PDPNPDPNPDPNPDPNP"
assert len(KIND) == NP
SPLIT = [j for j in range(NP) if KIND[j] != "N"]
NATIVE = [j for j in range(NP) if KIND[j] == "N"]
RING = 6
SLOT = [j % RING for j in range(NP0)] + [j % RING for j in range(NP1)]
assert NP0 <= RING and NP1 % RING == 0
GATHERS_PER_STEP = 7
LOOP_FROM = 5
assert LOOP_FROM % 2 == 1 and TILES % 2 == 0

PE_TRANSPOSE = 3
PE_LEFT = {MIX: 9, 0: 10, 1: 11, 2: 13, 3: 13, 4: 15, 5: 15}
PE_RIGHT = [13, 14, 16, 16, 1, 4, 7, 10]
ACT_ROWS = 0
ACT_HIGH_X = 6
ACT_LEFT = {MIX: 10, 0: 14, 1: 14, 2: 16, 3: 16, 4: NP, 5: NP}
ACT_RELU0 = 8
ACT_RELU1 = 3
DVE_LOW_Y = 9
DVE_LOW_X = 7
DVE_SUM1 = 5
DVE_SUM0 = 1
DVE_LATE = 1
LEFT_ORDER = [MIX, 0, 1, 2, 3, 4, 5]
PICK_RIGHT = {0: NA + 1, 1: NA + 2, 2: NA + 3, 3: NA + 4, "mix": NA + 5}
NPICK = NA + 6


def pair_index(s, j):
    if isinstance(s, int):
        if s == 0:
            return j
        if s == TILES:
            return NP * s - NP1 + j - NP0
    return s * NP + (j - NP1)


def count(kinds, s, j):
    n0 = sum(1 for x in range(NP0) if KIND[x] in kinds)
    n1 = sum(1 for x in range(NP0, NP) if KIND[x] in kinds)
    here = sum(1 for x in range(j + 1) if KIND[x] in kinds)
    if isinstance(s, int):
        if s == 0:
            return here
        if s == TILES:
            here -= n0
    return s * (n0 + n1) + (here - n1)


def group_index(s, g):
    if isinstance(s, int):
        if s == 0:
            return g
        if s == TILES:
            return NG * s - NGY + g - NGX
    return s * NG + (g - NGY)


def before(s, j, here):
    at = s if isinstance(s, int) else LOOP_FROM
    x, y = at, j
    while x >= 0:
        y -= 1
        if y < 0:
            x, y = x - 1, NP - 1
        if x >= 0 and present(x, y) and here(y):
            return pair_index(s, j) - (pair_index(at, j) - pair_index(x, y) - 1)
    return None


def present(s, j):
    if isinstance(s, int):
        return 0 <= s <= TILES and not (s == 0 and j >= NP0) and not (s == TILES and j < NP0)
    return True


def steps(engine, step):
    for s in range(-1, LOOP_FROM):
        step(s, s // 2, s % 2)
    with engine.Fori(0, (TILES - 1 - LOOP_FROM) // 2) as i:
        step(i * 2 + LOOP_FROM, i + LOOP_FROM // 2, 1)
        step(i * 2 + LOOP_FROM + 1, i + LOOP_FROM // 2 + 1, 0)
    for s in (TILES - 1, TILES):
        step(s, s // 2, s % 2)


def has(s, lo, hi):
    return not isinstance(s, int) or lo <= s <= hi


def build(nc, ids, dense, tables, w0, b0, w1, b1, wt1, bt1, wt2, bt2, wt3, pick_c, mix_rows_c, factors_c, out):
    with ExitStack() as ctx:
        def sb(name, shape, dt):
            return ctx.enter_context(nc.sbuf_tensor(name, shape, dt))

        def pb(name, shape, dt):
            return ctx.enter_context(nc.psum_tensor(name, shape, dt))

        def sem(name):
            return ctx.enter_context(nc.semaphore(name))

        mix_rows = sb("mix_rows", [P, 2], I32)
        factors = sb("factors", [P, 2], F32)
        idx = sb("idx", [P, NBLK, F], I32)
        rows = sb("rows", [P, F, NBLK * K], F32)
        rows_t = sb("rows_t", [P, KT, P], F32)
        ident = sb("ident", [P, P], F32)
        pick = sb("pick", [P, NPICK, P], F32R)
        xs = sb("xs", [P, COLS], F32R)
        left = sb("left", [P, 2 * NA + 1, COLS], F32)
        y = sb("y", [P, 2, COLS], F32)
        ys = sb("ys", [P, 2, COLS], F32R)
        z = sb("z", [P, 2, COLS], F32)
        prod = sb("prod", [P, RING, 2, COLS], F32)
        prod_hi = sb("prod_hi", [P, RING, 2, COLS], F32R)
        prod_lo = sb("prod_lo", [P, RING, 2, COLS], F32R)
        w_full = sb("w_full", [P, max(1, len(NATIVE)), 2, C], F32)
        w_hi = sb("w_hi", [P, len(SPLIT), 2, C], F32R)
        w_lo = sb("w_lo", [P, len(SPLIT), 2, C], F32R)
        sums0 = sb("sums0", [P, TILES // 2, P], F32)
        sums1 = sb("sums1", [P, TILES // 2, P], F32)
        bias0 = sb("bias0", [P, 1], F32)
        bias1 = sb("bias1", [P, 1], F32)
        top1 = sb("top1", [P, 2, N1], F32)
        top2 = sb("top2", [P, N1 // P, N2], F32)
        top3 = sb("top3", [P, N2 // P], F32)
        tbias1 = sb("tbias1", [P, N1 // P], F32)
        tbias2 = sb("tbias2", [P, N2 // P], F32)
        dense_in = sb("dense_in", [P, NBLK, DENSE], F32)
        h_in = sb("h_in", [P, 2, B], F32)
        h1 = left[:, 0:N1 // P, :]
        h2 = left[:, NA:NA + N2 // P, :]
        y_out = z[0:1, 0, :]
        pick_f = sums1[:, 0:NPICK, :]
        w0_fg = prod[:, 0:3].rearrange("p r e c -> p (r e c)")[:, 0:NA * NBX * C] \
            .rearrange("p (a b c) -> p a b c", a=NA, b=NBX)
        w0_gf = prod[:, 3:6].rearrange("p r e c -> p (r e c)")[:, 0:NA * NBX * C] \
            .rearrange("p (a b c) -> p a b c", a=NA, b=NBX)
        w1_fh = left[:, 0:NA].rearrange("p a c -> p (a c)").rearrange("p (a b c) -> p a b c", a=NA, b=NBY)
        w0_mix = left[:, NA, 0:2 * C].rearrange("p (o c) -> p o c", o=2)

        def weight(j):
            found = []
            for g, a in zip(*PAIRS[j]):
                of, b = RIGHT[g]
                found.append(w0_mix[:, 0, :] if a == MIX else (w0_fg if of == "x" else w1_fh)[:, a, b, :])
            return found

        acc0 = pb("acc0", [P, COLS], F32)
        acc1 = pb("acc1", [P, COLS], F32)
        right = pb("right", [P, BANKS, COLS], F32)
        stage = pb("stage", [P, 2, COLS], F32)

        ids_in = sem("ids_in")
        gathered = [sem(f"gathered{m}") for m in range(NBLK)]
        w_in = sem("w_in")
        mix_in = sem("mix_in")
        mix_w_in = sem("mix_w_in")
        factors_in = sem("factors_in")
        pick_in = sem("pick_in")
        small_in = sem("small_in")
        dense_inn = sem("dense_inn")
        consts = sem("consts")
        picks = sem("picks")
        pad0 = sem("pad0")
        w_sum = sem("w_sum")
        w_his = sem("w_his")
        w_los = sem("w_los")
        dense_t = sem("dense_t")
        dense_c = sem("dense_c")
        zeroed = sem("zeroed")
        tile_in = sem("tile_in")
        rows_t_ready = sem("rows_t_ready")
        transposed = sem("transposed")
        x_hi = sem("x_hi")
        x_lo = sem("x_lo")
        left_made = sem("left_made")
        left_ready = sem("left_ready")
        right_ready = sem("right_ready")
        multiplied = sem("multiplied")
        hi_ready = sem("hi_ready")
        lo_by_dve = sem("lo_by_dve")
        lo_by_pool = sem("lo_by_pool")
        contracted = sem("contracted")
        y_ready = sem("y_ready")
        y_hi = sem("y_hi")
        y_lo = sem("y_lo")
        z_ready = sem("z_ready")
        summed0 = sem("summed0")
        summed1 = sem("summed1")
        h_ready = sem("h_ready")
        top_mm = sem("top_mm")
        top_act = sem("top_act")
        stored = sem("stored")

        block = ctx.enter_context(nc.Block())
        W_DMAS = U * (2 * NBX + NBY)

        def load_weight(engine, dst, src, u, b):
            engine.dma_start(dst[V * u:V * (u + 1), :, b, :], src[u, b]).then_inc(w_in, 16)

        @block.sync
        def _(sp):
            sp.dma_start(idx[:], ids.rearrange("(m p) f -> p m f", p=P)).then_inc(ids_in, 16)
            sp.dma_start(mix_rows[:], mix_rows_c).then_inc(mix_in, 16)
            sp.dma_start(factors[:], factors_c).then_inc(factors_in, 16)
            sp.dma_start(pick_f, pick_c).then_inc(pick_in, 16)
            for u in range(U):
                for b in range(NBX):
                    load_weight(sp, w0_fg, w0.rearrange("(a u b v) c -> u b v a c", a=NA, u=U, b=NBX), u, b)
                    load_weight(sp, w0_gf, w0.rearrange("(b v a u) c -> u b v a c", b=NBX, v=V, a=NA), u, b)
            sp.dma_start(bias0[:], b0.rearrange("(p o) -> p o", o=1)).then_inc(small_in, 16)
            sp.dma_start(bias1[:], b1.rearrange("(p o) -> p o", o=1)).then_inc(small_in, 16)
            sp.dma_start(tbias1[:], bt1.rearrange("(p n) -> p n", p=P)).then_inc(small_in, 16)
            sp.dma_start(tbias2[:], bt2.rearrange("(p n) -> p n", p=P)).then_inc(small_in, 16)
            sp.dma_start(top3[:], wt3.rearrange("(p n) o -> p (n o)", p=P)).then_inc(small_in, 16)
            sp.dma_start(top2[:], wt2.rearrange("(p n) c -> p n c", p=P)).then_inc(small_in, 16)
            sp.dma_start(top1[:, 1, :], wt1[HID:HID + P, :]).then_inc(small_in, 16)
            sp.dma_start(dense_in[:], dense.rearrange("(m p) d -> p m d", p=P)).then_inc(dense_inn, 16)
            sp.wait_ge(zeroed, 1)
            sp.dma_start(top1[HID:P, 0, :], wt1[0:HID, :]).then_inc(small_in, 16)
            sp.dma_start(top1[0:DENSE, 0, :], wt1[HID + P:HID + P + DENSE, :]).then_inc(small_in, 16)
            sp.wait_ge(top_act, 3)
            sp.dma_start(out.rearrange("b o -> o b"), y_out).then_inc(stored, 16)
            sp.wait_ge(stored, 16)

        @block.gpsimd
        def _(pool):
            def gather(m, f):
                nc.gpsimd.indirect_dma_start(
                    rows[:, f, m * K:(m + 1) * K], None, tables[f],
                    bass.IndirectOffsetOnAxis(ap=idx[:, m, f:f + 1], axis=0)).then_inc(gathered[m], 16)

            pool.wait_ge(ids_in, 16)
            nc.gpsimd.memset(ident[:], 0.0).then_inc(consts, 1)
            pool.wait_ge(consts, 1)
            nc.gpsimd.affine_select(out=ident[:], in_=ident[:], compare_op=ALU.not_equal, fill=1.0, base=0,
                                    pattern=[[-1, P]], channel_multiplier=1).then_inc(consts, 1)
            pool.wait_ge(mix_in, 16)
            for f in range(F):
                gather(0, f)
                if f in (8, 9):
                    nc.gpsimd.indirect_dma_start(
                        w0_mix[:, f - 8, :], None, w0,
                        bass.IndirectOffsetOnAxis(ap=mix_rows[:, f - 8:f - 7], axis=0)).then_inc(mix_w_in, 16)

            def step(s, gathers=()):
                pairs = [j for j in range(NP) if KIND[j] == "P" and present(s, j)]
                gathers = list(gathers)
                for j in pairs:
                    for m, f in gathers[:1]:
                        gather(m, f)
                    gathers = gathers[1:]
                    pool.wait_ge(hi_ready, count("DP", s, j))
                    nc.gpsimd.tensor_tensor(prod_lo[:, SLOT[j]], prod[:, SLOT[j]],
                                            prod_hi[:, SLOT[j]].bitcast(F32), ALU.subtract) \
                        .then_inc(lo_by_pool, 1)
                for m, f in gathers:
                    gather(m, f)

            def admit():
                pool.sem_inc(tile_in, 1)

            pool.wait_ge(gathered[0], 16 * F)
            for t in range(P // (KT * NBLK)):
                admit()
            tiles_per_block = TILES // NBLK
            queue = [(m, f) for m in range(1, NBLK) for f in range(F)]
            last_gather_step = (NBLK - 1) * tiles_per_block
            for s in range(last_gather_step):
                m = s // tiles_per_block + 1
                mine = [q for q in queue if q[0] == m][:GATHERS_PER_STEP]
                queue = [q for q in queue if q not in mine]
                step(s, mine)
                if s % tiles_per_block == tiles_per_block - 2:
                    pool.wait_ge(gathered[m], 16 * F)
                    for t in range(tiles_per_block):
                        admit()
            assert not queue
            with pool.Fori(last_gather_step, TILES) as s:
                step(s)
            step(TILES)

        @block.tensor
        def _(pe):
            pe.wait_ge(consts, 2)
            pe.wait_ge(dense_inn, 16)
            for m in range(NBLK):
                last = nc.tensor.transpose(acc0[0:DENSE, m * P:(m + 1) * P], dense_in[:, m, :], ident[:])
            last.then_inc(dense_t, 1)
            pe.wait_ge(picks, 1)
            pe.wait_ge(w_his, 1)
            pe.wait_ge(w_los, 1)
            pe.wait_ge(dense_c, 1)

            def transpose(t):
                pe.wait_ge(rows_t_ready, t + 1)
                if has(t, 1, TILES):
                    pe.wait_ge(left_ready, t * (NA + 1) - 1)
                for k in range(KT):
                    last = nc.tensor.transpose(stage[:, 0, k * P:(k + 1) * P], rows_t[:, k, :], ident[:])
                last.then_inc(transposed, 1)

            def make_left(t, a):
                n = LEFT_ORDER.index(a)
                if n == 0:
                    pe.wait_ge(x_hi, t + 1)
                    pe.wait_ge(x_lo, t + 1)
                if n >= 2:
                    pe.wait_ge(left_ready, t * (NA + 1) + n - 1)
                elif n == 0 and has(t, 1, TILES):
                    pe.wait_ge(left_ready, t * (NA + 1))
                nc.tensor.matmul(stage[:, (1 + n) % 2, :], pick[:, a, :], xs[:], start=True, stop=True) \
                    .then_inc(left_made, 1)

            def make_right(s, par, g):
                done = before(s, FIRST[g], lambda j: any(x != g and (x - g) % BANKS == 0 for x in PAIRS[j][0]))
                if done is not None:
                    pe.wait_ge(multiplied, done)
                if g == NGX:
                    pe.wait_ge(y_hi, s)
                    pe.wait_ge(y_lo, s)
                src = xs[:] if g < NGX else ys[:, (par + 1) % 2, :]
                nc.tensor.matmul(right[:, g % BANKS, :], pick[:, PICK_RIGHT[RIGHT[g][1]], :], src,
                                 start=True, stop=True).then_inc(right_ready, 1)

            def contract(s, j):
                layer = int(j >= NP0)
                acc = (acc0, acc1)[layer][:]
                first, final = (j == 0, j == NP0 - 1) if layer == 0 else (j == NP0, j == NP - 1)
                if j == 0 and has(s, 1, TILES):
                    pe.wait_ge(y_ready, s)
                    pe.wait_ge(y_hi, s)
                if j == NP0 and has(s, 2, TILES):
                    pe.wait_ge(z_ready, s - 1)
                slot = SLOT[j]
                if KIND[j] == "N":
                    pe.wait_ge(multiplied, pair_index(s, j) + 1)
                    n = NATIVE.index(j)
                    for e in range(2):
                        last = nc.tensor.matmul(acc, w_full[:, n, e, :], prod[:, slot, e, :],
                                                start=(first and e == 0), stop=(final and e == 1))
                else:
                    n = SPLIT.index(j)
                    pe.wait_ge(hi_ready, count("DP", s, j))
                    for e in range(2):
                        nc.tensor.matmul(acc, w_hi[:, n, e, :], prod_hi[:, slot, e, :],
                                         start=(first and e == 0), stop=False)
                        nc.tensor.matmul(acc, w_lo[:, n, e, :], prod_hi[:, slot, e, :], start=False, stop=False)
                    if KIND[j] == "D":
                        pe.wait_ge(lo_by_dve, count("D", s, j))
                    else:
                        pe.wait_ge(lo_by_pool, count("P", s, j))
                    for e in range(2):
                        last = nc.tensor.matmul(acc, w_hi[:, n, e, :], prod_lo[:, slot, e, :],
                                                start=False, stop=(final and e == 1))
                last.then_inc(contracted, 1)

            def step(s, half, par):
                for j in range(NP):
                    for ahead in (0, 1):
                        t = s + ahead
                        if not has(t, 0, TILES - 1):
                            continue
                        here = j + NP * (1 - ahead)
                        if PE_TRANSPOSE == here:
                            transpose(t)
                        for a in LEFT_ORDER:
                            if PE_LEFT[a] == here:
                                make_left(t, a)
                        for g in range(NGX):
                            if PE_RIGHT[g] == here:
                                make_right(t, (par + ahead) % 2, g)
                    for g in range(NGX, NG):
                        if PE_RIGHT[g] == j and has(s, 1, TILES):
                            make_right(s, par, g)
                    if present(s, j):
                        contract(s, j)

            steps(pe, step)

            pe.wait_ge(small_in, 16 * 9)
            pe.wait_ge(h_ready, 3)
            banks = [acc0[:], acc1[:], stage[:, 0, :], stage[:, 1, :]]
            for n in range(N1 // P):
                for c in range(2):
                    last = nc.tensor.matmul(banks[n], top1[:, c, :].rearrange("p (m n) -> p n m", m=P)[:, n, :],
                                            h_in[:, c, :], start=(c == 0), stop=(c == 1))
            last.then_inc(top_mm, 1)
            pe.wait_ge(top_act, 1)
            for n in range(N2 // P):
                for c in range(N1 // P):
                    last = nc.tensor.matmul(right[:, n, :],
                                            top2[:, c, :].rearrange("p (m n) -> p n m", m=P)[:, n, :],
                                            h1[:, c, :], start=(c == 0), stop=(c == N1 // P - 1))
            last.then_inc(top_mm, 1)
            pe.wait_ge(top_act, 2)
            for c in range(N2 // P):
                last = nc.tensor.matmul(right[0:1, 2, :], top3[:, c:c + 1], h2[:, c, :],
                                        start=(c == 0), stop=(c == N2 // P - 1))
            last.then_inc(top_mm, 1)

        @block.vector
        def _(dve):
            nc.vector.memset(rows_t[:], 0.0).then_inc(pad0, 1)
            nc.vector.memset(top1[:, 0, :], 0.0)
            nc.vector.memset(h_in[:, 0, :], 0.0).then_inc(zeroed, 1)
            dve.wait_ge(pick_in, 16)
            nc.vector.tensor_copy(pick[:], pick_f).then_inc(picks, 1)
            dve.wait_ge(zeroed, 1)
            dve.wait_ge(dense_t, 1)
            nc.vector.tensor_copy(h_in[0:DENSE, 0, :], acc0[0:DENSE, :]).then_inc(dense_c, 1)
            dve.wait_ge(w_in, 16 * W_DMAS)
            for b in range(NBX):
                nc.vector.tensor_tensor(w0_fg[:, 0:2 * b + 1, b, :], w0_fg[:, 0:2 * b + 1, b, :],
                                        w0_gf[:, 0:2 * b + 1, b, :], ALU.add).then_inc(w_sum, 1)
            dve.wait_ge(mix_w_in, 32)
            nc.vector.tensor_tensor(w0_mix[:, 0, :], w0_mix[:, 0, :], w0_mix[:, 1, :], ALU.add).then_inc(w_sum, 1)
            dve.wait_ge(factors_in, 16)
            dve.wait_ge(w_sum, NBX + 1)
            for b in range(NBX):
                nc.vector.tensor_scalar(w0_fg[:, 2 * b, b, :], w0_fg[:, 2 * b, b, :], factors[:, 0:1], None,
                                        ALU.mult).then_inc(w_sum, 1)
            nc.vector.tensor_scalar(w0_mix[:, 0, :], w0_mix[:, 0, :], factors[:, 1:2], None, ALU.mult) \
                .then_inc(w_sum, 1)
            dve.wait_ge(w_his, 1)
            for n, j in enumerate(SPLIT):
                for e, w in enumerate(weight(j)):
                    last = nc.vector.tensor_tensor(w_lo[:, n, e, :], w, w_hi[:, n, e, :].bitcast(F32),
                                                   ALU.subtract)
            last.then_inc(w_los, 1)

            def low_x(t):
                dve.wait_ge(x_hi, t + 1)
                nc.vector.tensor_tensor(xs[HID:P, :], stage[0:HID, 0, :], xs[0:HID, :].bitcast(F32),
                                        ALU.subtract).then_inc(x_lo, 1)

            def low_y(s, par):
                dve.wait_ge(y_hi, s + 1)
                dve.wait_ge(y_ready, s + 1)
                nc.vector.tensor_tensor(ys[HID:P, par, :], y[0:HID, par, :], ys[0:HID, par, :].bitcast(F32),
                                        ALU.subtract).then_inc(y_lo, 1)

            def multiply(s, par, j):
                g, a = PAIRS[j]
                if j in FIRST:
                    dve.wait_ge(right_ready, group_index(s, max(g)) + 1)
                if j < NP0:
                    dve.wait_ge(left_ready, s * (NA + 1) + max(LEFT_ORDER.index(x) for x in a) + 1)
                free = before(s, j, lambda x: SLOT[x] == SLOT[j])
                if free is not None:
                    dve.wait_ge(contracted, free)
                t_par = par if j < NP0 else 1 - par
                at = [2 * NA if x == MIX else t_par * NA + x for x in a]
                x = g[0] % BANKS
                if g[0] == g[1]:
                    r = right[:, x, :].unsqueeze(1).broadcast_to([P, 2, COLS])
                else:
                    r = right[:, x:x + 2, :]
                nc.vector.tensor_tensor(prod[:, SLOT[j]], r, left[:, at[0]:at[1] + 1:at[1] - at[0], :],
                                        ALU.mult).then_inc(multiplied, 1)

            def low(s, j):
                dve.wait_ge(hi_ready, count("DP", s, j))
                nc.vector.tensor_tensor(prod_lo[:, SLOT[j]], prod[:, SLOT[j]],
                                        prod_hi[:, SLOT[j]].bitcast(F32), ALU.subtract).then_inc(lo_by_dve, 1)

            def sum_over_k(src, dst):
                return nc.vector.tensor_reduce(dst, src.rearrange("p t (k b) -> p b (t k)", k=KT), AX.X, ALU.add)

            def sum0(s, half):
                dve.wait_ge(y_ready, s)
                sum_over_k(y[HID:P], sums0[HID:P, bass.ds(half - 1, 1), :].rearrange("p o b -> p (o b)")) \
                    .then_inc(summed0, 1)

            def sum1(s, half):
                dve.wait_ge(z_ready, s - 1)
                sum_over_k(z[:], sums1[:, bass.ds(half - 1, 1), :].rearrange("p o b -> p (o b)")) \
                    .then_inc(summed1, 1)

            def step(s, half, par):
                late = []
                for j in range(NP):
                    if present(s, j):
                        multiply(s, par, j)
                    while late and (late[0] <= j - DVE_LATE or not present(s, j)):
                        low(s, late.pop(0))
                    if present(s, j) and KIND[j] == "D":
                        late.append(j)
                    if j == DVE_SUM0 and par == 0 and has(s, 2, TILES):
                        sum0(s, half)
                    if j == DVE_SUM1 and par == 1 and has(s, 3, TILES):
                        sum1(s, half)
                    if j == DVE_LOW_Y and has(s, 0, TILES - 1):
                        low_y(s, par)
                    if j == DVE_LOW_X and has(s, -1, TILES - 2):
                        low_x(s + 1)
                while late:
                    low(s, late.pop(0))

            steps(dve, step)

            per = TILES // 2 // NBLK
            dve.wait_ge(summed0, TILES // 2)
            dve.wait_ge(dense_c, 1)
            nc.vector.tensor_reduce(h_in[HID:P, 0, :].rearrange("p (m b) -> p m b", m=NBLK),
                                    sums0[HID:P].rearrange("p (m t) b -> p m b t", t=per),
                                    AX.X, ALU.add).then_inc(h_ready, 1)
            sum1(TILES + 1, TILES // 2)
            dve.wait_ge(summed1, TILES // 2)
            nc.vector.tensor_reduce(h_in[:, 1, :].rearrange("p (m b) -> p m b", m=NBLK),
                                    sums1[:].rearrange("p (m t) b -> p m b t", t=per),
                                    AX.X, ALU.add).then_inc(h_ready, 2)

        @block.scalar
        def _(act):
            for u in range(U):
                for b in range(NBY):
                    load_weight(act, w1_fh, w1.rearrange("(a u b v) c -> u b v a c", a=NA, u=U, b=NBY), u, b)
            act.wait_ge(w_sum, 2 * (NBX + 1))
            for j in range(NP):
                for e, w in enumerate(weight(j)):
                    if j in NATIVE:
                        last = nc.scalar.copy(w_full[:, NATIVE.index(j), e, :], w)
                    else:
                        last = nc.scalar.copy(w_hi[:, SPLIT.index(j), e, :], w)
            last.then_inc(w_his, 1)
            act.wait_ge(pad0, 1)
            act.wait_ge(small_in, 16 * 9)
            act.wait_ge(w_los, 1)

            def take_rows(t):
                act.wait_ge(tile_in, t + 1)
                if has(t, 1, TILES):
                    act.wait_ge(transposed, t)
                nc.scalar.copy(rows_t[:, :, 0:F],
                               rows[:, :, bass.ds(t * KT, KT)].rearrange("p f k -> p k f")) \
                    .then_inc(rows_t_ready, 1)

            def high_x(t):
                act.wait_ge(transposed, t + 1)
                if has(t, 1, TILES):
                    act.wait_ge(right_ready, group_index(t - 1, NGX - 1) + 1)
                nc.scalar.copy(xs[0:HID, :], stage[0:HID, 0, :]).then_inc(x_hi, 1)

            def store_left(t, par, a):
                n = LEFT_ORDER.index(a)
                act.wait_ge(left_made, t * (NA + 1) + n + 1)
                if a == MIX:
                    if has(t, 1, TILES):
                        act.wait_ge(multiplied, pair_index(t - 1, NP0 - 1) + 1)
                elif has(t, 2, TILES):
                    act.wait_ge(multiplied, pair_index(t - 1, NP - NA // 2 + a // 2) + 1)
                at = 2 * NA if a == MIX else par * NA + a
                nc.scalar.copy(left[:, at, :], stage[:, (1 + n) % 2, :]).then_inc(left_ready, 1)

            def high(s, j):
                act.wait_ge(multiplied, pair_index(s, j) + 1)
                nc.scalar.copy(prod_hi[:, SLOT[j]], prod[:, SLOT[j]]).then_inc(hi_ready, 1)

            def relu0(s, half, par):
                act.wait_ge(contracted, pair_index(s, NP0 - 1) + 1)
                if has(s, 2, TILES):
                    act.wait_ge(summed0, half)
                    act.wait_ge(right_ready, group_index(s - 1, NG - 1) + 1)
                    act.wait_ge(y_lo, s - 1)
                nc.scalar.activation(ys[0:HID, par, :], acc0[0:HID, :], ACT.Relu, bias=bias0[0:HID]) \
                    .then_inc(y_hi, 1)
                nc.scalar.activation(y[:, par, :], acc0[:], ACT.Relu, bias=bias0[:]).then_inc(y_ready, 1)

            def relu1(s, half, par):
                act.wait_ge(contracted, pair_index(s - 1, NP - 1) + 1)
                if has(s, 4, TILES + 1):
                    act.wait_ge(summed1, half - 1)
                nc.scalar.activation(z[:, par, :], acc1[:], ACT.Relu, bias=bias1[:]).then_inc(z_ready, 1)

            def step(s, half, par):
                for j in range(NP):
                    if KIND[j] != "N" and present(s, j):
                        high(s, j)
                    if j == ACT_RELU1 and has(s, 2, TILES):
                        relu1(s, half, par)
                    if j == ACT_RELU0 and has(s, 0, TILES - 1):
                        relu0(s, half, par)
                    for ahead in (0, 1):
                        t = s + ahead
                        if not has(t, 0, TILES - 1):
                            continue
                        here = j + NP * (1 - ahead)
                        if ACT_ROWS == here:
                            take_rows(t)
                        if ACT_HIGH_X == here:
                            high_x(t)
                        for a in LEFT_ORDER:
                            if ACT_LEFT[a] == here:
                                store_left(t, (par + ahead) % 2, a)

            steps(act, step)
            relu1(TILES + 1, (TILES + 1) // 2, (TILES + 1) % 2)

            banks = [acc0[:], acc1[:], stage[:, 0, :], stage[:, 1, :]]
            act.wait_ge(top_mm, 1)
            for n in range(N1 // P):
                last = nc.scalar.activation(h1[:, n, :], banks[n], ACT.Relu, bias=tbias1[:, n:n + 1])
            last.then_inc(top_act, 1)
            act.wait_ge(top_mm, 2)
            for n in range(N2 // P):
                last = nc.scalar.activation(h2[:, n, :], right[:, n, :], ACT.Relu, bias=tbias2[:, n:n + 1])
            last.then_inc(top_act, 1)
            act.wait_ge(top_mm, 3)
            nc.scalar.copy(y_out, right[0:1, 2, :]).then_inc(top_act, 1)


def constants():
    picks = np.zeros((P, NPICK, P), np.float32)
    mix_rows = np.zeros((P, 2), np.int32)
    factors = np.ones((P, 2), np.float32)

    def set_pick(n, p, feature):
        picks[feature, n, p] = picks[HID + feature, n, p] = 1.0

    for p in range(P):
        for a in range(NA):
            set_pick(a, p, U * a + p // V)
        for b in range(NBY):
            set_pick(PICK_RIGHT[b], p, V * b + p % V)
        d, i, block = p // (U * NBX), p // NBX % U, p % NBX
        if d < SHIFTS:
            f, g = V * block + U + i, V * block + U + (i + d) % U
            set_pick(MIX, p, f)
            set_pick(PICK_RIGHT["mix"], p, g)
            mix_rows[p] = f * F + g, g * F + f
            factors[p, 1] = 0.5 if d in (0, U // 2) else 1.0
        factors[p, 0] = 0.5 if p % V < U else 1.0
    return picks, mix_rows, factors


def kernel(**inputs):
    import concourse.bacc as bacc
    from concourse.bass_utils import run_bass_kernel_spmd

    nc = bacc.Bacc("TRN2", target_bir_lowering=False, num_devices=1)
    arrays = {}

    def put(name, a=None):
        a = np.ascontiguousarray(inputs[name] if a is None else a)
        arrays["in_" + name] = a
        return nc.dram_tensor("in_" + name, a.shape, mybir.dt.from_np(a.dtype), kind="ExternalInput").ap()

    out = nc.dram_tensor("out_y", (B, 1), F32, kind="ExternalOutput").ap()
    tables = [put(f"tbl_{f}") for f in range(F)]
    picks, mix_rows, factors = constants()
    build(nc, put("ids"), put("dense_ctx"), tables, put("L0_rec_W0"), put("L0_rec_b0"), put("L0_rec_W1"),
          put("L0_rec_b1"), put("W_top1"), put("b_top1"), put("W_top2"), put("b_top2"), put("W_top3"),
          put("picks", picks), put("mix_rows", mix_rows), put("factors", factors), out)
    r = run_bass_kernel_spmd(nc, [arrays], core_ids=[0])
    return r.results[0]["out_y"]
```

```python
import numpy as np
from contextlib import ExitStack

import concourse.bass as bass
from concourse import mybir

F32 = mybir.dt.float32
F32R = mybir.dt.float32r
I32 = mybir.dt.int32
ALU = mybir.AluOpType
ACT = mybir.ActivationFunctionType
AX = mybir.AxisListType

B, F, K, C = 512, 48, 32, 128
HID = C // 2
DENSE = 16
N1, N2 = 512, 256
P = 128
TOP_CHUNKS = (N1 + N2) // P
NBLK = B // P
KT = 4
COLS = KT * P
TILES = B * K // COLS
U, V = 8, 16
NA = F // U
NBX, NBY = F // V, HID // V
MIX = NA
SHIFTS = U // 2 + 1
MIX_RUNS = [(d * U * NBX + i * NBX, n, V // 2 + i, V // 2 + (i + d) % U)
            for d in range(SHIFTS) for i, n in ((0, U - d), (U - d, d)) if n]

RIGHT = [("x", 1), ("x", 2), ("x", 0), ("x", "mix"), ("y", 0), ("y", 1), ("y", 2), ("y", 3)]
NG, NGX, NGY = len(RIGHT), NBX + 1, NBY
BANKS = 4
assert NGX % BANKS == 0 and NGY % BANKS == 0
PAIRS0 = [((0, 0), (0, 1)), ((0, 1), (2, 3)), ((1, 1), (0, 1)), ((1, 1), (2, 4)), ((2, 3), (0, MIX))]
PAIRS1 = [((NGX + b, NGX + b), (2 * i, 2 * i + 1)) for b in range(NBY) for i in range(NA // 2)]
PAIRS = PAIRS0 + PAIRS1
NP0, NP1, NP = len(PAIRS0), len(PAIRS1), len(PAIRS)
FIRST = [min(j for j in range(NP) if g in PAIRS[j][0]) for g in range(NG)]
LAST = [max(j for j in range(NP) if g in PAIRS[j][0]) for g in range(NG)]
KIND = "PDPNPDPNPDNNPNPDP"
assert len(KIND) == NP
SPLIT = [j for j in range(NP) if KIND[j] != "N"]
NATIVE = [j for j in range(NP) if KIND[j] == "N"]
RING = 6
SLOT = [j % RING for j in range(NP0)] + [j % RING for j in range(NP1)]
assert NP0 <= RING and NP1 % RING == 0
GATHERS_PER_STEP = 7
ROW_BLOCKS = 2
TPB = TILES // NBLK
LEFTS = 3
SP_LOOP_FROM = 5
LOOP_FROM = 5
assert LOOP_FROM % 2 == 1 and TILES % 2 == 0 and (TILES - SP_LOOP_FROM) % LEFTS == 0 and SP_LOOP_FROM >= LEFTS

PE_TRANSPOSE = 3
PE_JOIN_X = 5
PE_MIX = 5
PE_RIGHT = [11, 11, 17, 16, 0, 4, 4, 8]
ACT_ROWS = 0
ACT_SPLIT_X = 4
ACT_STORE_X = 7
ACT_MIX = 13
ACT_RELU0 = 10
ACT_RELU1 = 3
DVE_LOW_Y = 15
DVE_LOW_ROWS = 2
DVE_SUM1 = 4
DVE_SUM0 = 0
DVE_LATE = 2
PE_RIGHT_TILE_1 = [3, 3, 4, 5]
PE_MIX_TILE_1 = 2
DVE_LOW_Y_TILE_0 = 2
PICK_RIGHT = {0: 0, 1: 1, 2: 2, 3: 3, "mix": 4}
PICK_MIX = 5
PICK_X = 6
PICK_ALL = 7
NPICK = 8


def pair_index(s, j):
    if isinstance(s, int):
        if s == 0:
            return j
        if s == TILES:
            return NP * s - NP1 + j - NP0
    return s * NP + (j - NP1)


def count(kinds, s, j):
    n0 = sum(1 for x in range(NP0) if KIND[x] in kinds)
    n1 = sum(1 for x in range(NP0, NP) if KIND[x] in kinds)
    here = sum(1 for x in range(j + 1) if KIND[x] in kinds)
    if isinstance(s, int):
        if s == 0:
            return here
        if s == TILES:
            here -= n0
    return s * (n0 + n1) + (here - n1)


def group_index(s, g):
    if isinstance(s, int):
        if s == 0:
            return g
        if s == TILES:
            return NG * s - NGY + g - NGX
    return s * NG + (g - NGY)


def before(s, j, here):
    at = s if isinstance(s, int) else LOOP_FROM
    x, y = at, j
    while x >= 0:
        y -= 1
        if y < 0:
            x, y = x - 1, NP - 1
        if x >= 0 and present(x, y) and here(y):
            return pair_index(s, j) - (pair_index(at, j) - pair_index(x, y) - 1)
    return None


def present(s, j):
    if isinstance(s, int):
        return 0 <= s <= TILES and not (s == 0 and j >= NP0) and not (s == TILES and j < NP0)
    return True


def steps(engine, step):
    for s in range(-1, LOOP_FROM):
        step(s, s // 2, s % 2)
    with engine.Fori(0, (TILES - 1 - LOOP_FROM) // 2) as i:
        step(i * 2 + LOOP_FROM, i + LOOP_FROM // 2, 1)
        step(i * 2 + LOOP_FROM + 1, i + LOOP_FROM // 2 + 1, 0)
    for s in (TILES - 1, TILES):
        step(s, s // 2, s % 2)


def has(s, lo, hi):
    return not isinstance(s, int) or lo <= s <= hi


def build(nc, ids, dense, tables, w0, b0, w1, b1, wt1, bt1, wt2, bt2, wt3, pick_c, factors_c, out):
    with ExitStack() as ctx:
        def sb(name, shape, dt):
            return ctx.enter_context(nc.sbuf_tensor(name, shape, dt))

        def pb(name, shape, dt):
            return ctx.enter_context(nc.psum_tensor(name, shape, dt))

        def sem(name):
            return ctx.enter_context(nc.semaphore(name))

        factors = sb("factors", [P, 2], F32)
        idx = sb("idx", [P, NBLK, F], I32)
        rows = sb("rows", [P, F, ROW_BLOCKS * K], F32)
        rows_t = sb("rows_t", [P, KT, 2, HID], F32R)
        ident = sb("ident", [P, P], F32)
        pick = sb("pick", [P, NPICK, P], F32R)
        xs = sb("xs", [P, COLS], F32R)
        x_full = sb("x_full", [HID, COLS], F32)
        left = sb("left", [P, LEFTS * NA, COLS], F32)
        left_mix = sb("left_mix", [P, COLS], F32)
        y = sb("y", [P, 2, COLS], F32)
        ys = sb("ys", [P, 2, COLS], F32R)
        z = sb("z", [P, 2, COLS], F32)
        prod = sb("prod", [P, RING, 2, COLS], F32)
        prod_hi = sb("prod_hi", [P, RING, 2, COLS], F32R)
        prod_lo = sb("prod_lo", [P, RING, 2, COLS], F32R)
        w_full = sb("w_full", [P, max(1, len(NATIVE)), 2, C], F32)
        w_hi = sb("w_hi", [P, len(SPLIT), 2, C], F32R)
        w_lo = sb("w_lo", [P, len(SPLIT), 2, C], F32R)
        sums0 = sb("sums0", [P, TILES // 2, P], F32)
        sums1 = sb("sums1", [P, TILES // 2, P], F32)
        bias0 = sb("bias0", [P, 1], F32)
        bias1 = sb("bias1", [P, 1], F32)
        top1 = sb("top1", [P, 2, N1], F32)
        top2 = sb("top2", [P, N1 // P, N2], F32)
        top3 = sb("top3", [P, N2 // P], F32)
        tbias1 = sb("tbias1", [P, N1 // P], F32)
        tbias2 = sb("tbias2", [P, N2 // P], F32)
        dense_in = sb("dense_in", [P, NBLK, DENSE], F32)
        h_in = sb("h_in", [P, 2, B], F32)
        h1 = left[:, 0:N1 // P, :]
        h2 = left[:, NA:NA + N2 // P, :]
        y_out = z[0:1, 0, :]
        pick_f = sums1[:, 0:NPICK, :]
        w0_fg = prod[:, 0:3].rearrange("p r e c -> p (r e c)")[:, 0:NA * NBX * C] \
            .rearrange("p (a b c) -> p a b c", a=NA, b=NBX)
        w0_gf = prod[:, 3:6].rearrange("p r e c -> p (r e c)")[:, 0:NA * NBX * C] \
            .rearrange("p (a b c) -> p a b c", a=NA, b=NBX)
        w1_fh = left[:, 0:NA].rearrange("p a c -> p (a c)").rearrange("p (a b c) -> p a b c", a=NA, b=NBY)
        w0_mix = left[:, NA, 0:2 * C].rearrange("p (o c) -> p o c", o=2)

        def tile_rows(t):
            return rows[:, :, bass.ds(t % (ROW_BLOCKS * TPB) * KT, KT)].rearrange("p f k -> p k f")

        def weight(j):
            found = []
            for g, a in zip(*PAIRS[j]):
                of, b = RIGHT[g]
                found.append(w0_mix[:, 0, :] if a == MIX else (w0_fg if of == "x" else w1_fh)[:, a, b, :])
            return found

        acc0 = pb("acc0", [P, COLS], F32)
        acc1 = pb("acc1", [P, COLS], F32)
        right = pb("right", [P, BANKS, COLS], F32)
        stage = pb("stage", [P, 2, COLS], F32)

        ids_in = sem("ids_in")
        gathered = [sem(f"gathered{m}") for m in range(NBLK)]
        x_stored = sem("x_stored")
        x_saved = sem("x_saved")
        left_in = sem("left_in")
        w0_in = sem("w0_in")
        w1_in = sem("w1_in")
        mix_zero = sem("mix_zero")
        mix_w_in = sem("mix_w_in")
        factors_in = sem("factors_in")
        pick_in = sem("pick_in")
        small_in = sem("small_in")
        dense_inn = sem("dense_inn")
        consts = sem("consts")
        picks = sem("picks")
        pad0 = sem("pad0")
        w_sum = sem("w_sum")
        w_copied = sem("w_copied")
        bias_in = sem("bias_in")
        w_los = sem("w_los")
        dense_t = sem("dense_t")
        dense_c = sem("dense_c")
        zeroed = sem("zeroed")
        tile_in = sem("tile_in")
        rows_hi = sem("rows_hi")
        rows_lo = sem("rows_lo")
        transposed = sem("transposed")
        x_split = sem("x_split")
        x_joined = sem("x_joined")
        mix_made = sem("mix_made")
        mix_ready = sem("mix_ready")
        right_ready = sem("right_ready")
        multiplied = sem("multiplied")
        hi_ready = sem("hi_ready")
        lo_by_dve = sem("lo_by_dve")
        lo_by_pool = sem("lo_by_pool")
        contracted = sem("contracted")
        y_ready = sem("y_ready")
        y_hi = sem("y_hi")
        y_lo = sem("y_lo")
        z_ready = sem("z_ready")
        summed0 = sem("summed0")
        summed1 = sem("summed1")
        h_ready = sem("h_ready")
        top_mm = sem("top_mm")
        top_act = sem("top_act")
        stored = sem("stored")

        block = ctx.enter_context(nc.Block())
        x_dram = nc.dram_tensor("x_dram", (LEFTS, F, COLS), F32, kind="Internal").ap()
        W0_DMAS = 2 * sum(2 * b + 1 for b in range(NBX))
        W1_DMAS = NA * NBY

        @block.sync
        def _(sp):
            sp.dma_start(idx[:], ids.rearrange("(m p) f -> p m f", p=P)).then_inc(ids_in, 16)
            sp.dma_start(factors[:], factors_c).then_inc(factors_in, 16)
            sp.dma_start(pick_f, pick_c).then_inc(pick_in, 16)
            sp.dma_start(dense_in[:], dense.rearrange("(m p) d -> p m d", p=P)).then_inc(dense_inn, 16)
            for b in range(NBX):
                for a in range(2 * b + 1):
                    sp.dma_start(w0_fg[:, a, b, :], w0.rearrange("(a u b v) c -> a b v u c", a=NA, u=U, b=NBX)[a, b]) \
                        .then_inc(w0_in, 16)
                    sp.dma_start(w0_gf[:, a, b, :], w0.rearrange("(b v a u) c -> a b v u c", b=NBX, v=V, a=NA)[a, b]) \
                        .then_inc(w0_in, 16)
            sp.dma_start(bias0[:], b0.rearrange("(p o) -> p o", o=1)).then_inc(bias_in, 16)
            sp.dma_start(bias1[:], b1.rearrange("(p o) -> p o", o=1)).then_inc(bias_in, 16)
            sp.dma_start(tbias1[:], bt1.rearrange("(p n) -> p n", p=P)).then_inc(small_in, 16)
            sp.dma_start(tbias2[:], bt2.rearrange("(p n) -> p n", p=P)).then_inc(small_in, 16)
            sp.dma_start(top3[:], wt3.rearrange("(p n) o -> p (n o)", p=P)).then_inc(small_in, 16)
            sp.dma_start(top2[:], wt2.rearrange("(p n) c -> p n c", p=P)).then_inc(small_in, 16)
            sp.dma_start(top1[:, 1, :], wt1[HID:HID + P, :]).then_inc(small_in, 16)
            sp.wait_ge(zeroed, 1)
            sp.dma_start(top1[HID:P, 0, :], wt1[0:HID, :]).then_inc(small_in, 16)
            sp.dma_start(top1[0:DENSE, 0, :], wt1[HID + P:HID + P + DENSE, :]).then_inc(small_in, 16)

            def save_and_copy(tile, slot, first=False):
                sp.wait_ge(x_stored, tile(1, 1))
                sp.dma_start(x_dram[slot], x_full[0:F, :]).then_inc(x_saved, 16)
                sp.wait_ge(x_saved, tile(16, 16))
                if first:
                    sp.wait_ge(left_in, 16 * NA)
                for a in range(NA):
                    sp.dma_start(left[:, slot * NA + a, :],
                                 x_dram[slot, U * a:U * (a + 1), :].unsqueeze(0).broadcast_to([V, U, COLS])) \
                        .then_inc(left_in, 16)

            for t in range(SP_LOOP_FROM):
                save_and_copy(lambda a, b, t=t: a * t + b, t % LEFTS, t == 1)
            with sp.Fori(0, (TILES - SP_LOOP_FROM) // LEFTS) as i:
                for n in range(LEFTS):
                    save_and_copy(lambda a, b, n=n: i * (a * LEFTS) + (a * (SP_LOOP_FROM + n) + b),
                                  (SP_LOOP_FROM + n) % LEFTS)
            sp.wait_ge(top_act, TOP_CHUNKS + 1)
            sp.dma_start(out.rearrange("b o -> o b"), y_out).then_inc(stored, 16)
            sp.wait_ge(stored, 16)

        @block.gpsimd
        def _(pool):
            def gather(m, f):
                nc.gpsimd.indirect_dma_start(
                    rows[:, f, m % ROW_BLOCKS * K:(m % ROW_BLOCKS + 1) * K], None, tables[f],
                    bass.IndirectOffsetOnAxis(ap=idx[:, m, f:f + 1], axis=0)).then_inc(gathered[m], 16)

            pool.wait_ge(ids_in, 16)
            nc.gpsimd.memset(ident[:], 0.0).then_inc(consts, 1)
            pool.wait_ge(consts, 1)
            nc.gpsimd.affine_select(out=ident[:], in_=ident[:], compare_op=ALU.not_equal, fill=1.0, base=0,
                                    pattern=[[-1, P]], channel_multiplier=1).then_inc(consts, 1)
            for f in range(F):
                gather(0, f)

            def step(s, gathers=()):
                pairs = [j for j in range(NP) if KIND[j] == "P" and present(s, j)]
                gathers = list(gathers)
                for j in pairs:
                    for m, f in gathers[:1]:
                        gather(m, f)
                    gathers = gathers[1:]
                    pool.wait_ge(hi_ready, count("DP", s, j))
                    nc.gpsimd.tensor_tensor(prod_lo[:, SLOT[j]], prod[:, SLOT[j]],
                                            prod_hi[:, SLOT[j]].bitcast(F32), ALU.subtract) \
                        .then_inc(lo_by_pool, 1)
                for m, f in gathers:
                    gather(m, f)

            def admit():
                pool.sem_inc(tile_in, 1)

            pool.wait_ge(gathered[0], 16 * F)
            for t in range(TPB):
                admit()
            queue = [(m, f) for m in range(1, NBLK) for f in range(F)]
            last_gather_step = (NBLK - 1) * TPB
            for s in range(last_gather_step):
                m = s // TPB + 1
                mine = [q for q in queue if q[0] == m][:GATHERS_PER_STEP]
                queue = [q for q in queue if q not in mine]
                if mine and mine[0][1] == 0 and m >= ROW_BLOCKS:
                    pool.wait_ge(rows_lo, (m - ROW_BLOCKS + 1) * TPB)
                step(s, mine)
                if s % TPB == TPB - 2:
                    pool.wait_ge(gathered[m], 16 * F)
                    for t in range(TPB):
                        admit()
            assert not queue
            with pool.Fori(last_gather_step, TILES) as s:
                step(s)
            step(TILES)

        @block.tensor
        def _(pe):
            pe.wait_ge(consts, 2)
            pe.wait_ge(dense_inn, 16)
            for m in range(NBLK):
                last = nc.tensor.transpose(acc0[0:DENSE, m * P:(m + 1) * P], dense_in[:, m, :], ident[:])
            last.then_inc(dense_t, 1)
            pe.wait_ge(picks, 1)
            pe.wait_ge(w_copied, 2 * NP)
            pe.wait_ge(w_los, 1)
            pe.wait_ge(dense_c, 1)

            def transpose(t):
                pe.wait_ge(rows_lo, t + 1)
                if has(t, 1, TILES):
                    pe.wait_ge(x_stored, t)
                for k in range(KT):
                    last = nc.tensor.matmul(stage[:, 0, k * P:(k + 1) * P],
                                            rows_t[:, k].rearrange("p h f -> p (h f)"), pick[:, PICK_ALL, :],
                                            start=True, stop=True)
                last.then_inc(transposed, 1)

            def join_x(t):
                pe.wait_ge(x_split, t + 1)
                nc.tensor.matmul(stage[:, 0, :], pick[:, PICK_X, :], xs[:], start=True, stop=True) \
                    .then_inc(x_joined, 1)

            def make_mix(t):
                pe.wait_ge(x_split, t + 1)
                if has(t, 1, TILES):
                    pe.wait_ge(mix_ready, t)
                nc.tensor.matmul(stage[:, 1, :], pick[:, PICK_MIX, :], xs[:], start=True, stop=True) \
                    .then_inc(mix_made, 1)

            def make_right(s, par, g):
                done = before(s, FIRST[g], lambda j: any(x != g and (x - g) % BANKS == 0 for x in PAIRS[j][0]))
                if isinstance(s, int) and s == 1 and g < NGX:
                    done = LAST[g] + 1
                if done is not None:
                    pe.wait_ge(multiplied, done)
                if g == NGX:
                    pe.wait_ge(y_hi, s)
                    pe.wait_ge(y_lo, s)
                src = xs[:] if g < NGX else ys[:, (par + 1) % 2, :]
                nc.tensor.matmul(right[:, g % BANKS, :], pick[:, PICK_RIGHT[RIGHT[g][1]], :], src,
                                 start=True, stop=True).then_inc(right_ready, 1)

            def contract(s, j):
                layer = int(j >= NP0)
                acc = (acc0, acc1)[layer][:]
                first, final = (j == 0, j == NP0 - 1) if layer == 0 else (j == NP0, j == NP - 1)
                if j == 0 and has(s, 1, TILES):
                    pe.wait_ge(y_ready, s)
                    pe.wait_ge(y_hi, s)
                if j == NP0 and has(s, 2, TILES):
                    pe.wait_ge(z_ready, s - 1)
                slot = SLOT[j]
                if KIND[j] == "N":
                    pe.wait_ge(multiplied, pair_index(s, j) + 1)
                    n = NATIVE.index(j)
                    for e in range(2):
                        last = nc.tensor.matmul(acc, w_full[:, n, e, :], prod[:, slot, e, :],
                                                start=(first and e == 0), stop=(final and e == 1))
                else:
                    n = SPLIT.index(j)
                    pe.wait_ge(hi_ready, count("DP", s, j))
                    for e in range(2):
                        nc.tensor.matmul(acc, w_hi[:, n, e, :], prod_hi[:, slot, e, :],
                                         start=(first and e == 0), stop=False)
                        nc.tensor.matmul(acc, w_lo[:, n, e, :], prod_hi[:, slot, e, :], start=False, stop=False)
                    if KIND[j] == "D":
                        pe.wait_ge(lo_by_dve, count("D", s, j))
                    else:
                        pe.wait_ge(lo_by_pool, count("P", s, j))
                    for e in range(2):
                        last = nc.tensor.matmul(acc, w_hi[:, n, e, :], prod_lo[:, slot, e, :],
                                                start=False, stop=(final and e == 1))
                last.then_inc(contracted, 1)

            def step(s, half, par):
                for j in range(NP):
                    for ahead in (0, 1):
                        t = s + ahead
                        if not has(t, 0, TILES - 1):
                            continue
                        here = j + NP * (1 - ahead)
                        if PE_TRANSPOSE == here and has(t, 2, TILES):
                            transpose(t)
                        if PE_JOIN_X == here and has(t, 2, TILES):
                            join_x(t)
                        place = PE_MIX_TILE_1 if isinstance(t, int) and t == 1 else PE_MIX
                        if place == here and has(t, 1, TILES):
                            make_mix(t)
                        for g in range(NGX):
                            place = PE_RIGHT_TILE_1[g] if isinstance(t, int) and t == 1 else PE_RIGHT[g]
                            if place == here and has(t, 1, TILES):
                                make_right(t, (par + ahead) % 2, g)
                    for g in range(NGX, NG):
                        if PE_RIGHT[g] == j and has(s, 1, TILES):
                            make_right(s, par, g)
                    if present(s, j):
                        contract(s, j)

            transpose(0)
            join_x(0)
            make_mix(0)
            for g in range(NGX):
                make_right(0, 0, g)
            transpose(1)
            join_x(1)
            steps(pe, step)

            pe.wait_ge(small_in, 16 * 7)
            for c in range(2):
                pe.wait_ge(h_ready, (1, 3)[c])
                for n in range(N1 // P):
                    last = nc.tensor.matmul(right[:, n, :], top1[:, c, :].rearrange("p (m n) -> p n m", m=P)[:, n, :],
                                            h_in[:, c, :], start=(c == 0), stop=(c == 1))
                    if c == 1:
                        last.then_inc(top_mm, 1)
            banks = [acc0[:], stage[:, 0, :]]
            for c in range(N1 // P):
                pe.wait_ge(top_act, c + 1)
                for n in range(N2 // P):
                    last = nc.tensor.matmul(banks[n], top2[:, c, :].rearrange("p (m n) -> p n m", m=P)[:, n, :],
                                            h1[:, c, :], start=(c == 0), stop=(c == N1 // P - 1))
                    if c == N1 // P - 1:
                        last.then_inc(top_mm, 1)
            for c in range(N2 // P):
                pe.wait_ge(top_act, N1 // P + c + 1)
                last = nc.tensor.matmul(stage[0:1, 1, :], top3[:, c:c + 1], h2[:, c, :],
                                        start=(c == 0), stop=(c == N2 // P - 1))
            last.then_inc(top_mm, 1)

        @block.vector
        def _(dve):
            nc.vector.memset(w0_mix, 0.0).then_inc(mix_zero, 1)
            nc.vector.memset(rows_t[:].bitcast(F32), 0.0).then_inc(pad0, 1)
            nc.vector.memset(top1[:, 0, :], 0.0)
            nc.vector.memset(h_in[:, 0, :], 0.0).then_inc(zeroed, 1)
            dve.wait_ge(pick_in, 16)
            nc.vector.tensor_copy(pick[:], pick_f).then_inc(picks, 1)
            dve.wait_ge(zeroed, 1)
            dve.wait_ge(dense_t, 1)
            nc.vector.tensor_copy(h_in[0:DENSE, 0, :], acc0[0:DENSE, :]).then_inc(dense_c, 1)
            dve.wait_ge(w0_in, 16 * W0_DMAS)
            for b in range(NBX):
                nc.vector.tensor_tensor(w0_fg[:, 0:2 * b + 1, b, :], w0_fg[:, 0:2 * b + 1, b, :],
                                        w0_gf[:, 0:2 * b + 1, b, :], ALU.add).then_inc(w_sum, 1)
            dve.wait_ge(mix_w_in, 16 * 2 * len(MIX_RUNS))
            nc.vector.tensor_tensor(w0_mix[:, 0, :], w0_mix[:, 0, :], w0_mix[:, 1, :], ALU.add).then_inc(w_sum, 1)
            dve.wait_ge(factors_in, 16)
            dve.wait_ge(w_sum, NBX + 1)
            for b in range(NBX):
                nc.vector.tensor_scalar(w0_fg[:, 2 * b, b, :], w0_fg[:, 2 * b, b, :], factors[:, 0:1], None,
                                        ALU.mult).then_inc(w_sum, 1)
            nc.vector.tensor_scalar(w0_mix[:, 0, :], w0_mix[:, 0, :], factors[:, 1:2], None, ALU.mult) \
                .then_inc(w_sum, 1)
            for n, j in enumerate(SPLIT):
                if n == SPLIT.index(min(x for x in SPLIT if x >= NP0)):
                    dve.wait_ge(w1_in, 16 * W1_DMAS)
                dve.wait_ge(w_copied, 2 * (j + 1))
                for e, w in enumerate(weight(j)):
                    last = nc.vector.tensor_tensor(w_lo[:, n, e, :], w, w_hi[:, n, e, :].bitcast(F32),
                                                   ALU.subtract)
            last.then_inc(w_los, 1)

            def low_rows(t):
                dve.wait_ge(rows_hi, t + 1)
                nc.vector.tensor_tensor(rows_t[:, :, 1, 0:F], tile_rows(t), rows_t[:, :, 0, 0:F].bitcast(F32),
                                        ALU.subtract).then_inc(rows_lo, 1)

            def low_y(s, par):
                dve.wait_ge(y_hi, s + 1)
                dve.wait_ge(y_ready, s + 1)
                nc.vector.tensor_tensor(ys[HID:P, par, :], y[0:HID, par, :], ys[0:HID, par, :].bitcast(F32),
                                        ALU.subtract).then_inc(y_lo, 1)

            def multiply(s, lb, j):
                g, a = PAIRS[j]
                if j in FIRST:
                    dve.wait_ge(right_ready, group_index(s, max(g)) + 1)
                if j == 0:
                    dve.wait_ge(left_in, 16 * NA * (s + 1))
                if MIX in a:
                    dve.wait_ge(mix_ready, s + 1)
                free = before(s, j, lambda x: SLOT[x] == SLOT[j])
                if free is not None:
                    dve.wait_ge(contracted, free)
                if MIX in a:
                    for e in range(2):
                        last = nc.vector.tensor_tensor(
                            prod[:, SLOT[j], e, :], right[:, g[e] % BANKS, :],
                            left_mix[:] if a[e] == MIX else one(left, lb[0] * NA + a[e]), ALU.mult)
                    last.then_inc(multiplied, 1)
                    return
                x = g[0] % BANKS
                if g[0] == g[1]:
                    r = right[:, x, :].unsqueeze(1).broadcast_to([P, 2, COLS])
                else:
                    r = right[:, x:x + 2, :]
                two = left[:, bass.ds(lb[j >= NP0] * NA + a[0], 2, a[1] - a[0]), :]
                nc.vector.tensor_tensor(prod[:, SLOT[j]], r, two, ALU.mult).then_inc(multiplied, 1)

            def one(tensor, n):
                return tensor[:, bass.ds(n, 1), :].rearrange("p o c -> p (o c)")

            def low(s, j):
                dve.wait_ge(hi_ready, count("DP", s, j))
                nc.vector.tensor_tensor(prod_lo[:, SLOT[j]], prod[:, SLOT[j]],
                                        prod_hi[:, SLOT[j]].bitcast(F32), ALU.subtract).then_inc(lo_by_dve, 1)

            def sum_over_k(src, dst):
                return nc.vector.tensor_reduce(dst, src.rearrange("p t (k b) -> p b (t k)", k=KT), AX.X, ALU.add)

            def sum0(s, half):
                dve.wait_ge(y_ready, s)
                sum_over_k(y[HID:P], sums0[HID:P, bass.ds(half - 1, 1), :].rearrange("p o b -> p (o b)")) \
                    .then_inc(summed0, 1)

            def sum1(s, half):
                dve.wait_ge(z_ready, s - 1)
                sum_over_k(z[:], sums1[:, bass.ds(half - 1, 1), :].rearrange("p o b -> p (o b)")) \
                    .then_inc(summed1, 1)

            def step(s, half, par):
                late = []
                lb = (s % LEFTS, (s + LEFTS - 1) % LEFTS)
                for j in range(NP):
                    if present(s, j):
                        multiply(s, lb, j)
                    while late and (late[0] <= j - DVE_LATE or not present(s, j)):
                        low(s, late.pop(0))
                    if present(s, j) and KIND[j] == "D":
                        late.append(j)
                    if j == DVE_SUM0 and par == 0 and has(s, 2, TILES):
                        sum0(s, half)
                    if j == DVE_SUM1 and par == 1 and has(s, 3, TILES):
                        sum1(s, half)
                    if j == DVE_LOW_Y_TILE_0 and isinstance(s, int) and s == 1:
                        low_y(0, 0)
                    if j == DVE_LOW_Y and has(s, 1, TILES - 1):
                        low_y(s, par)
                    if j == DVE_LOW_ROWS and has(s, 1, TILES - 2):
                        low_rows(s + 1)
                while late:
                    low(s, late.pop(0))

            low_rows(0)
            low_rows(1)
            steps(dve, step)

            per = TILES // 2 // NBLK
            dve.wait_ge(summed0, TILES // 2)
            dve.wait_ge(dense_c, 1)
            nc.vector.tensor_reduce(h_in[HID:P, 0, :].rearrange("p (m b) -> p m b", m=NBLK),
                                    sums0[HID:P].rearrange("p (m t) b -> p m b t", t=per),
                                    AX.X, ALU.add).then_inc(h_ready, 1)
            dve.wait_ge(summed1, TILES // 2 - per)
            nc.vector.tensor_reduce(h_in[:, 1, 0:B - P].rearrange("p (m b) -> p m b", m=NBLK - 1),
                                    sums1[:, 0:TILES // 2 - per].rearrange("p (m t) b -> p m b t", t=per),
                                    AX.X, ALU.add).then_inc(h_ready, 1)
            sum1(TILES + 1, TILES // 2)
            dve.wait_ge(summed1, TILES // 2)
            nc.vector.tensor_reduce(h_in[:, 1, B - P:B], sums1[:, TILES // 2 - per:].rearrange("p t b -> p b t"),
                                    AX.X, ALU.add).then_inc(h_ready, 1)

        @block.scalar
        def _(act):
            act.wait_ge(mix_zero, 1)
            for o in range(2):
                for p, n, f, g in MIX_RUNS:
                    row = (f * F + g, g * F + f)[o]
                    act.dma_start(w0_mix[p:p + NBX * n, o, :],
                                  bass.AP(w0.tensor, w0.offset + row * C,
                                          [[(F + 1) * C, n], [V * (F + 1) * C, NBX], [1, C]])).then_inc(mix_w_in, 16)
            for b in range(NBY):
                for a in range(NA):
                    act.dma_start(w1_fh[:, a, b, :], w1.rearrange("(a u b v) c -> a b v u c", a=NA, u=U, b=NBY)[a, b]) \
                        .then_inc(w1_in, 16)
            act.wait_ge(w_sum, 2 * (NBX + 1))
            for j in range(NP):
                if j == NP0:
                    act.wait_ge(w1_in, 16 * W1_DMAS)
                for e, w in enumerate(weight(j)):
                    if j in NATIVE:
                        nc.scalar.copy(w_full[:, NATIVE.index(j), e, :], w).then_inc(w_copied, 1)
                    else:
                        nc.scalar.copy(w_hi[:, SPLIT.index(j), e, :], w).then_inc(w_copied, 1)
            act.wait_ge(pad0, 1)
            act.wait_ge(bias_in, 16 * 2)
            act.wait_ge(w_los, 1)

            def take_rows(t):
                act.wait_ge(tile_in, t + 1)
                if has(t, 1, TILES):
                    act.wait_ge(transposed, t)
                nc.scalar.copy(rows_t[:, :, 0, 0:F], tile_rows(t)).then_inc(rows_hi, 1)

            def split_x(t):
                act.wait_ge(transposed, t + 1)
                if has(t, 1, TILES):
                    act.wait_ge(right_ready, group_index(t - 1, NGX - 1) + 1)
                nc.scalar.copy(xs[:], stage[:, 0, :]).then_inc(x_split, 1)

            def store_x(t):
                act.wait_ge(x_joined, t + 1)
                if has(t, 1, TILES):
                    act.wait_ge(x_saved, 16 * t)
                nc.scalar.copy(x_full[:], stage[0:HID, 0, :]).then_inc(x_stored, 1)

            def store_mix(t):
                act.wait_ge(mix_made, t + 1)
                if has(t, 1, TILES):
                    act.wait_ge(multiplied, pair_index(t - 1, NP0 - 1) + 1)
                nc.scalar.copy(left_mix[:], stage[:, 1, :]).then_inc(mix_ready, 1)

            def high(s, j):
                act.wait_ge(multiplied, pair_index(s, j) + 1)
                nc.scalar.copy(prod_hi[:, SLOT[j]], prod[:, SLOT[j]]).then_inc(hi_ready, 1)

            def relu0(s, half, par):
                act.wait_ge(contracted, pair_index(s, NP0 - 1) + 1)
                if has(s, 2, TILES):
                    act.wait_ge(summed0, half)
                    act.wait_ge(right_ready, group_index(s - 1, NG - 1) + 1)
                    act.wait_ge(y_lo, s - 1)
                nc.scalar.activation(ys[0:HID, par, :], acc0[0:HID, :], ACT.Relu, bias=bias0[0:HID]) \
                    .then_inc(y_hi, 1)
                nc.scalar.activation(y[:, par, :], acc0[:], ACT.Relu, bias=bias0[:]).then_inc(y_ready, 1)

            def relu1(s, half, par):
                act.wait_ge(contracted, pair_index(s - 1, NP - 1) + 1)
                if has(s, 4, TILES + 1):
                    act.wait_ge(summed1, half - 1)
                nc.scalar.activation(z[:, par, :], acc1[:], ACT.Relu, bias=bias1[:]).then_inc(z_ready, 1)

            def step(s, half, par):
                for j in range(NP):
                    if KIND[j] != "N" and present(s, j):
                        high(s, j)
                    if j == ACT_RELU1 and has(s, 2, TILES):
                        relu1(s, half, par)
                    if j == 0 and isinstance(s, int) and s == 1:
                        relu0(0, 0, 0)
                    if j == ACT_RELU0 and has(s, 1, TILES - 1):
                        relu0(s, half, par)
                    for ahead in (0, 1):
                        t = s + ahead
                        if not has(t, 0, TILES - 1):
                            continue
                        here = j + NP * (1 - ahead)
                        if ACT_ROWS == here and has(t, 2, TILES):
                            take_rows(t)
                        if ACT_SPLIT_X == here and has(t, 2, TILES):
                            split_x(t)
                        if ACT_STORE_X == here and has(t, 2, TILES):
                            store_x(t)
                        if ACT_MIX == here:
                            store_mix(t)

            for t in (0, 1):
                take_rows(t)
                split_x(t)
                store_x(t)
            steps(act, step)
            relu1(TILES + 1, (TILES + 1) // 2, (TILES + 1) % 2)

            act.wait_ge(small_in, 16 * 7)
            for n in range(N1 // P):
                act.wait_ge(top_mm, n + 1)
                nc.scalar.activation(h1[:, n, :], right[:, n, :], ACT.Relu, bias=tbias1[:, n:n + 1]) \
                    .then_inc(top_act, 1)
            for n, bank in enumerate((acc0[:], stage[:, 0, :])):
                act.wait_ge(top_mm, N1 // P + n + 1)
                nc.scalar.activation(h2[:, n, :], bank, ACT.Relu, bias=tbias2[:, n:n + 1]).then_inc(top_act, 1)
            act.wait_ge(top_mm, TOP_CHUNKS + 1)
            nc.scalar.copy(y_out, stage[0:1, 1, :]).then_inc(top_act, 1)


def constants():
    picks = np.zeros((P, NPICK, P), np.float32)
    factors = np.ones((P, 2), np.float32)

    def set_pick(n, p, feature):
        picks[feature, n, p] = picks[HID + feature, n, p] = 1.0

    for p in range(P):
        for b in range(NBY):
            set_pick(PICK_RIGHT[b], p, V * b + p // U)
        picks[p, PICK_ALL, p] = 1.0
        if p < F:
            set_pick(PICK_X, p, p)
        d, i, block = p // (U * NBX), p // NBX % U, p % NBX
        if d < SHIFTS:
            f, g = V * block + U + i, V * block + U + (i + d) % U
            set_pick(PICK_MIX, p, f)
            set_pick(PICK_RIGHT["mix"], p, g)
            factors[p, 1] = 0.5 if d in (0, U // 2) else 1.0
        factors[p, 0] = 0.5 if p // U < U else 1.0
    return picks, factors


def kernel(**inputs):
    import concourse.bacc as bacc
    from concourse.bass_utils import run_bass_kernel_spmd

    nc = bacc.Bacc("TRN2", target_bir_lowering=False, num_devices=1)
    arrays = {}

    def put(name, a=None):
        a = np.ascontiguousarray(inputs[name] if a is None else a)
        arrays["in_" + name] = a
        return nc.dram_tensor("in_" + name, a.shape, mybir.dt.from_np(a.dtype), kind="ExternalInput").ap()

    out = nc.dram_tensor("out_y", (B, 1), F32, kind="ExternalOutput").ap()
    tables = [put(f"tbl_{f}") for f in range(F)]
    picks, factors = constants()
    build(nc, put("ids"), put("dense_ctx"), tables, put("L0_rec_W0"), put("L0_rec_b0"), put("L0_rec_W1"),
          put("L0_rec_b1"), put("W_top1"), put("b_top1"), put("W_top2"), put("b_top2"), put("W_top3"),
          put("picks", picks), put("factors", factors), out)
    r = run_bass_kernel_spmd(nc, [arrays], core_ids=[0])
    return r.results[0]["out_y"]
```
